# Optimizing a Trainium2 kernel written in Bass

```python
import numpy as np
import jax
import jax.numpy as jnp

def _softmax(x, axis=-1):
    return jax.nn.softmax(x, axis=axis)

def _gelu(x):
    return jax.nn.gelu(x, approximate=True)

def _silu(x):
    return jax.nn.silu(x)

def _sigmoid(x):
    return jax.nn.sigmoid(x)

def _layernorm(x, axis=-1, eps=1e-05):
    m = jnp.mean(x, axis=axis, keepdims=True)
    v = jnp.var(x, axis=axis, keepdims=True)
    return (x - m) / jnp.sqrt(v + eps)

def _scatter_add(tgt, idx, src, axis=0):
    return tgt.at[idx].add(src)

def _segment_sum(src, seg, n):
    return jax.ops.segment_sum(src, seg, n)
kernel_name = 'mk_gnn_preln_d1_gnn_r8_08bc4e'

def setup_inputs(seed: int=0):
    np.random.seed(seed)
    _w = jnp.asarray

    def _rec_inputs():
        import jax
        import jax.numpy as jnp
        _gk = jax.random.key(seed)
        x = -0.0003713 + 1 * jax.random.normal(jax.random.fold_in(_gk, 1), (12500, 128), jnp.float32)
        _s = jax.random.randint(jax.random.fold_in(_gk, 2), (200000,), 0, 12500, jnp.int32)
        _d = jax.random.randint(jax.random.fold_in(_gk, 3), (200000,), 0, 12500, jnp.int32)
        _loop = jnp.arange(12500, dtype=jnp.int32)
        src = jnp.concatenate([_s, _d, _loop])
        dst = jnp.concatenate([_d, _s, _loop])
        _o = jnp.argsort(dst, stable=True)
        src = src[_o]
        dst = dst[_o]
        edge_attr_48 = -4.21973e-05 + 0.999841 * jax.random.normal(jax.random.fold_in(_gk, 12), (412500, 48), jnp.float32)
        return (x, src, dst, edge_attr_48)
    x, src, dst, edge_attr_48 = _rec_inputs()

    def _L0_gnn_setup():
        import jax, jax.numpy as jnp
        import numpy as np
        N_NODES = 12500
        N_EDGES = 200000
        NODE_DIM = 128
        EDGE_DIM = 48
        GLOBAL_DIM = 64
        N_GRAPHS = 64
        HIDDEN = 256
        key = jax.random.key(seed)
        ks = jax.random.split(key, 9)
        nodes = jax.random.normal(ks[0], (N_NODES, NODE_DIM), dtype=jnp.float32)
        edges = jax.random.normal(ks[1], (N_EDGES, EDGE_DIM), dtype=jnp.float32)
        edge_index = jax.random.randint(ks[2], (2, N_EDGES), 0, N_NODES, dtype=jnp.int64)
        batch = jnp.sort(jax.random.randint(ks[3], (N_NODES,), 0, N_GRAPHS, dtype=jnp.int64))
        graph_globals = jax.random.normal(ks[4], (N_GRAPHS, GLOBAL_DIM), dtype=jnp.float32)
        in_dim = NODE_DIM + EDGE_DIM + GLOBAL_DIM
        s1 = 1.0 / np.sqrt(in_dim)
        s2 = 1.0 / np.sqrt(HIDDEN)
        W1 = jax.random.uniform(ks[5], (in_dim, HIDDEN), minval=-s1, maxval=s1, dtype=jnp.float32)
        b1 = jax.random.uniform(ks[6], (HIDDEN,), minval=-s1, maxval=s1, dtype=jnp.float32)
        W2 = jax.random.uniform(ks[7], (HIDDEN, NODE_DIM), minval=-s2, maxval=s2, dtype=jnp.float32)
        b2 = jax.random.uniform(ks[8], (NODE_DIM,), minval=-s2, maxval=s2, dtype=jnp.float32)
        return {'nodes': nodes, 'edges': edges, 'edge_index': edge_index, 'batch': batch, 'graph_globals': graph_globals, 'W1': W1, 'b1': b1, 'W2': W2, 'b2': b2}
    _L0_gnn_all = _L0_gnn_setup()
    _L0_gnn_in = {k: v for k, v in _L0_gnn_all.items() if k in ('graph_globals', 'W1', 'b1', 'W2', 'b2')}
    del _L0_gnn_all
    return {'x': x, 'src': src, 'dst': dst, 'edge_attr_48': edge_attr_48, 'L0_gnn_graph_globals': _L0_gnn_in['graph_globals'], 'L0_gnn_W1': _L0_gnn_in['W1'], 'L0_gnn_b1': _L0_gnn_in['b1'], 'L0_gnn_W2': _L0_gnn_in['W2'], 'L0_gnn_b2': _L0_gnn_in['b2']}

def reference(x, src, dst, edge_attr_48, L0_gnn_graph_globals, L0_gnn_W1, L0_gnn_b1, L0_gnn_W2, L0_gnn_b2):
    import jax
    import jax.numpy as jnp

    def _L0_gnn_ref(nodes, edges, edge_index, batch, graph_globals, W1, b1, W2, b2):
        import jax, jax.numpy as jnp
        import numpy as np
        N_NODES = 12500
        N_EDGES = 200000
        NODE_DIM = 128
        EDGE_DIM = 48
        GLOBAL_DIM = 64
        N_GRAPHS = 64
        HIDDEN = 256
        recv = edge_index[1]
        agg = jax.ops.segment_sum(edges, recv, num_segments=N_NODES)
        u = graph_globals[batch]
        x = jnp.concatenate([nodes, agg, u], axis=1)
        h = jax.nn.relu(x @ W1 + b1)
        return h @ W2 + b2
    edge_index = jnp.stack([src, dst])
    batch0 = jnp.zeros((12500,), jnp.int32)
    h = jnp.maximum(_layernorm(x, axis=-1), 0.0)
    x = x + _L0_gnn_ref(h, edge_attr_48, edge_index, batch0, L0_gnn_graph_globals, L0_gnn_W1, L0_gnn_b1, L0_gnn_W2, L0_gnn_b2)
    return x

_drawn_inputs = setup_inputs


def setup_inputs(seed=0):
    import zlib

    import numpy as np

    out = dict(_drawn_inputs(seed))
    spreads = {}
    factors = {'L0_gnn_b1': 4.149}
    for name, (base, spread) in spreads.items():
        noise = np.random.default_rng([zlib.crc32(name.encode()), seed]).standard_normal(out[name].shape)
        drawn = base * np.exp(spread * noise) if base else spread * noise
        out[name] = jnp.asarray(drawn.astype(out[name].dtype))
    for name, factor in factors.items():
        out[name] = (out[name] * factor).astype(out[name].dtype)
    return out
```

```python
import concourse.bass as bass
from concourse import mybir
from contextlib import ExitStack

P = 128
EDGES_PER_ROW = 6
WINDOW = 32
GROUPS = 11
QUADS = ((0, 4), (4, 4), (8, 3))
QUAD_WINDOW = ((0, 104), (84, 196), (176, 276))
STEP_WINDOW = 276
TILE = 256
LAG = 3
F_NODE, F_EDGE, F_GLOBAL, HIDDEN = 128, 48, 64, 256
GENERAL_BLOCK = 512
EPS = 1e-5


class At:

    def __init__(self, c, i=0):
        self.c, self.i = c, i

    @property
    def value(self):
        return self.i * 2 + self.c if not isinstance(self.i, int) else self.c + 2 * self.i

    @property
    def parity(self):
        return self.c % 2

    @property
    def half(self):
        return self.i + self.c // 2

    def plus(self, n):
        return At(self.c + n, self.i)


def gnn_kernel(nc, x, dst, edges, graph_globals, w1, b1, w2, b2, out):
    fp32, i32 = mybir.dt.float32, mybir.dt.int32
    ALU = mybir.AluOpType
    ACT = mybir.ActivationFunctionType
    AX = mybir.AxisListType

    nodes, n_edges = x.shape[0], edges.shape[0]
    group_edges = P * EDGES_PER_ROW
    step_edges = group_edges * GROUPS
    steps = -(-n_edges // step_edges)
    tiles = -(-nodes // TILE)
    last_edge0 = n_edges - step_edges
    repeated = steps * step_edges - n_edges
    last_node0 = nodes - TILE
    fresh_row = (tiles * TILE - nodes) // 2
    masked_row = (repeated - group_edges) // EDGES_PER_ROW
    assert group_edges < repeated < 2 * group_edges and repeated % EDGES_PER_ROW == 0
    assert (tiles * TILE - nodes) % 2 == 0 and steps == tiles and steps % 2 == 1 and steps >= 7
    ROW = EDGES_PER_ROW * F_EDGE
    STEP_COLS = GROUPS * EDGES_PER_ROW
    n_groups = steps * GROUPS
    blocks = -(-n_groups // P)
    blocks_g = -(-nodes // GENERAL_BLOCK)
    agg_cols = max(blocks_g * GENERAL_BLOCK, nodes + STEP_WINDOW)

    ctx = ExitStack()
    with ctx:
        def sb(name, shape, dt=fp32):
            return ctx.enter_context(nc.sbuf_tensor(name, shape, dt))

        def bank(name):
            return ctx.enter_context(nc.psum_tensor(name, [P, 512], fp32))

        def sem(name):
            return ctx.enter_context(nc.semaphore(name))

        edge_buf = [sb(f"edge_buf{p}", [P, GROUPS, ROW]) for p in range(2)]
        onehot = [sb(f"onehot{p}", [P, STEP_COLS, WINDOW]) for p in range(2)]
        group_sums = [sb(f"group_sums{p}", [P, 3 * F_EDGE]) for p in range(2)]
        placing = [sb(f"placing{p}", [P, 3, 112]) for p in range(2)]
        agg = sb("agg", [F_EDGE, agg_cols])
        dst_rows = sb("dst_rows", [P, blocks, group_edges + 1], i32)
        rel_rows = sb("rel_rows", [P, blocks, group_edges])
        order_scrap = sb("order_scrap", [P, group_edges])
        rel = sb("rel", [P, blocks * P * EDGES_PER_ROW])
        first_i = sb("first_i", [steps, GROUPS], i32)
        last_i = sb("last_i", [steps, GROUPS], i32)
        first_f = sb("first_f", [steps, GROUPS + 1])
        last_f = sb("last_f", [steps, GROUPS])
        first_rel = sb("first_rel", [steps, GROUPS + 1])
        last_rel = sb("last_rel", [steps, GROUPS])
        tests = sb("tests", [steps, 6, GROUPS])
        low_limit = sb("low_limit", [steps, GROUPS])
        high_limit = sb("high_limit", [steps, GROUPS])
        final_node = sb("final_node", [steps, 1])
        spread = sb("spread", [steps, 3, 4, WINDOW])
        position = sb("position", [P, 3 * steps])
        step_base_i = sb("step_base_i", [1, steps], i32)
        step_base_f = sb("step_base_f", [1, steps])
        base_floor = sb("base_floor", [1, steps])
        step_base = sb("step_base", [1, steps], i32)
        violation = sb("violation", [P, blocks + 1])
        worst = sb("worst", [P, 1])
        worst_all = sb("worst_all", [P, 1])
        general_flag = sb("general_flag", [1, 1], i32)
        ramp = sb("ramp", [P, STEP_WINDOW])
        ones = sb("ones", [P, P])
        ident = sb("ident", [P, P])
        zeros = sb("zeros", [1, GENERAL_BLOCK])
        w1_node = sb("w1_node", [F_NODE, HIDDEN])
        w1_edge = sb("w1_edge", [F_EDGE, HIDDEN])
        w1_global = sb("w1_global", [F_GLOBAL, HIDDEN])
        w2_sb = sb("w2_sb", [P, 2, F_NODE])
        global_col = sb("global_col", [F_GLOBAL, 1])
        b1_col = sb("b1_col", [P, 2])
        hidden_bias = sb("hidden_bias", [P, 2])
        b2_rows = sb("b2_rows", [P, 2, F_NODE])
        eps_col = sb("eps_col", [P, 1])
        x_buf = [sb(f"x_buf{p}", [P, 2, F_NODE]) for p in range(2)]
        xb_buf = [sb(f"xb_buf{p}", [P, 2, F_NODE]) for p in range(2)]
        out_buf = [sb(f"out_buf{p}", [P, 2, F_NODE]) for p in range(2)]
        bn6 = sb("bn6", [P, 2, 6])
        mean_var = sb("mean_var", [P, 2, 2])
        deviation = sb("deviation", [P, 2])
        inverse = sb("inverse", [P, 2])
        shift = sb("shift", [P, 2])
        normed_x = sb("normed_x", [P, 2, F_NODE])
        normed_t = sb("normed_t", [P, TILE])
        hidden = sb("hidden", [P, 2, TILE])
        general_edges = sb("general_edges", [P, ROW])
        general_dst = sb("general_dst", [P, GROUPS, EDGES_PER_ROW], i32)
        general_rel = sb("general_rel", [P, STEP_COLS])
        general_onehot = sb("general_onehot", [P, EDGES_PER_ROW, GENERAL_BLOCK])
        general_ramp = sb("general_ramp", [P, GENERAL_BLOCK])

        group_bank = [bank(f"group_bank{p}") for p in range(2)]
        window_bank = [bank(f"window_bank{p}") for p in range(2)]
        turned_bank, out_bank = bank("turned_bank"), bank("out_bank")
        hidden_bank = [bank(f"hidden_bank{c}") for c in range(2)]

        dst_in = [sem(f"dst_in{b}") for b in range(blocks)]
        tables_in = sem("tables_in")
        weights_in = sem("weights_in")
        edges_in = [[sem(f"edges_in{p}{q}") for q in range(3)] for p in range(2)]
        x_in = [sem(f"x_in{p}") for p in range(2)]
        stored = [sem(f"stored{p}") for p in range(2)]
        consts_ready = sem("consts_ready")
        ident_ready = sem("ident_ready")
        agg_zeroed = sem("agg_zeroed")
        rel_rows_ready = sem("rel_rows_ready")
        rel_turned = sem("rel_turned")
        rel_ready = sem("rel_ready")
        tables_ready = sem("tables_ready")
        spread_ready = sem("spread_ready")
        position_turned = sem("position_turned")
        position_ready = sem("position_ready")
        bias_summed = sem("bias_summed")
        bias_ready = sem("bias_ready")
        setup_chain = sem("setup_chain")
        onehot_ready = sem("onehot_ready")
        edges_used = sem("edges_used")
        sums_copied = sem("sums_copied")
        placing_ready = sem("placing_ready")
        window_ready = sem("window_ready")
        agg_added = sem("agg_added")
        moments_halfway = sem("moments_halfway")
        moments_ready = sem("moments_ready")
        deviation_ready = sem("deviation_ready")
        inverse_ready = sem("inverse_ready")
        shift_ready = sem("shift_ready")
        normed = sem("normed")
        x_turned = sem("x_turned")
        turned_copied = sem("turned_copied")
        hidden_ready = sem("hidden_ready")
        hidden_copied = sem("hidden_copied")
        out_ready = sem("out_ready")
        xb_ready = sem("xb_ready")
        out_added = sem("out_added")
        worst_ready = sem("worst_ready")
        worst_shared = sem("worst_shared")
        flag_ready = sem("flag_ready")
        general_edges_in = sem("general_edges_in")
        general_dst_in = sem("general_dst_in")
        general_rel_chain = sem("general_rel_chain")
        general_rel_ready = sem("general_rel_ready")
        general_staged = sem("general_staged")
        general_used = sem("general_used")
        general_summed = sem("general_summed")
        general_added = sem("general_added")

        edge_view = edges.rearrange("e d -> (e d)")

        def tile_node0(m):
            if isinstance(m.i, int) and m.value == tiles - 1:
                return last_node0
            return m.value * TILE

        def step_edge0(t):
            if isinstance(t.i, int) and t.value == steps - 1:
                return last_edge0
            return t.value * step_edges

        def pairs(eng, first, count, body):
            if count >= 2:
                with eng.Fori(0, count // 2) as i:
                    body(At(first, i))
                    body(At(first + 1, i))
            if count % 2:
                body(At(first + count - 1))

        ctx.enter_context(nc.allow_non_contiguous_dma(reason="a few small columns of dst, biases"))
        block = ctx.enter_context(nc.Block())

        @block.sync
        def _(sp):
            def load_dst(b):
                first = b * P * group_edges
                rows = min(P, n_groups - GROUPS - b * P)
                if rows > 0:
                    sp.dma_start(dst_rows[0:rows, b, :], bass.AP(
                        tensor=dst.tensor, offset=first, ap=[[group_edges, rows], [1, group_edges + 1]]))\
                        .then_inc(dst_in[b], 16)
                if b == blocks - 1:
                    rows = max(rows, 0)
                    sp.dma_start(dst_rows[rows:rows + GROUPS - 1, b, :], bass.AP(
                        tensor=dst.tensor, offset=last_edge0,
                        ap=[[group_edges, GROUPS - 1], [1, group_edges + 1]])).then_inc(dst_in[b], 16)
                    rows += GROUPS - 1
                    sp.dma_start(dst_rows[rows:rows + 1, b, 0:group_edges],
                                 dst[n_edges - group_edges:].rearrange("(g e) -> g e", g=1))\
                        .then_inc(dst_in[b], 16)
                    sp.dma_start(dst_rows[rows:rows + 1, b, group_edges:],
                                 dst[n_edges - 1:].rearrange("(g e) -> g e", e=1)).then_inc(dst_in[b], 16)

            def load_edges(t):
                e0 = step_edge0(t)
                for q, (g0, ng) in enumerate(QUADS):
                    if not (isinstance(t.i, int) and t.value < 2):
                        sp.wait_ge(edges_used, 3 * t.plus(-2).value + q + 1)
                    n = ng * group_edges * F_EDGE
                    src = edge_view[bass.ds((e0 + g0 * group_edges) * F_EDGE, n)]
                    sp.dma_start(edge_buf[t.parity][:, g0:g0 + ng, :],
                                 src.rearrange("(g p d) -> p g d", g=ng, p=P))\
                      .then_inc(edges_in[t.parity][q], 16)

            def load_x(k, m):
                if not (isinstance(k.i, int) and k.value < 2):
                    sp.wait_ge(normed, k.plus(-1).value)
                    sp.wait_ge(xb_ready, k.plus(-1).value)
                sp.dma_start(x_buf[k.parity][:, :, :], x[bass.ds(tile_node0(m), TILE), :]
                             .rearrange("(p j) f -> p j f", j=2)).then_inc(x_in[k.parity], 16)

            def store(k, m):
                sp.wait_ge(out_added, k.plus(1).value)
                row = fresh_row if isinstance(m.i, int) and m.value == tiles - 1 else 0
                first = tile_node0(m) + 2 * row
                sp.dma_start(out[bass.ds(first, TILE - 2 * row), :].rearrange("(p j) f -> p j f", j=2),
                             out_buf[k.parity][row:, :, :]).then_inc(stored[k.parity], 16)

            def column(t, first, rows, stride, cols, col_stride):
                return bass.AP(tensor=t.tensor, offset=first, ap=[[stride, rows], [col_stride, cols]])

            load_dst(0)
            for table, first in ((first_i, 0), (last_i, group_edges - 1)):
                sp.dma_start(table[0:steps - 1, :], column(dst, first, steps - 1, step_edges, GROUPS,
                                                           group_edges)).then_inc(tables_in, 16)
                sp.dma_start(table[steps - 1:steps, :], column(dst, last_edge0 + first, 1, 1, GROUPS,
                                                               group_edges)).then_inc(tables_in, 16)
            sp.dma_start(step_base_i[0:1, 0:steps - 1], column(dst, 0, 1, 1, steps - 1, step_edges))\
              .then_inc(tables_in, 16)
            sp.dma_start(step_base_i[0:1, steps - 1:], column(dst, last_edge0, 1, 1, 1, 1))\
              .then_inc(tables_in, 16)
            load_edges(At(0))
            load_x(At(0), At(0))
            for b in range(1, blocks):
                load_dst(b)
            load_edges(At(1))
            load_x(At(1), At(1))

            def step(s):
                if not (isinstance(s.i, int) and s.value < 4):
                    store(s.plus(-4), s.plus(-4))
                if not (isinstance(s.i, int) and (s.value < 3 or s.value - 1 >= tiles)):
                    load_x(s.plus(-1), s.plus(-1))
                if not (isinstance(s.i, int) and s.value + 2 >= steps):
                    load_edges(s.plus(2))

            for s in range(4):
                step(At(s))
            pairs(sp, 4, steps - 7, step)
            for s in range(steps - 3, tiles + 4):
                step(At(s))
            sp.wait_ge(stored[0], 16 * ((tiles + 1) // 2))
            sp.wait_ge(stored[1], 16 * (tiles // 2))

            sp.wait_ge(flag_ready, 1)
            flag = sp.value_load(general_flag[0:1, 0:1], min_val=0, max_val=1)
            with sp.If(flag > 0):
                def load_chunk(b, c, edge0):
                    n = b * steps + c
                    sp.wait_ge(general_used, n * GROUPS + 1)
                    src = edge_view[bass.ds(edge0 * F_EDGE, step_edges * F_EDGE)]
                    sp.dma_start(edge_buf[0][:, :, :], src.rearrange("(g p d) -> p g d", g=GROUPS, p=P))\
                      .then_inc(general_edges_in, 16)
                    sp.dma_start(general_dst[:, :, :], dst[bass.ds(edge0, step_edges)]
                                 .rearrange("(g p r) -> p g r", g=GROUPS, p=P)).then_inc(general_dst_in, 16)

                with sp.Fori(0, blocks_g) as b:
                    with sp.Fori(0, steps - 1) as c:
                        load_chunk(b, c, c * step_edges)
                    load_chunk(b, steps - 1, last_edge0)

                def tile(m):
                    load_x(m.plus(tiles), m)
                    store(m.plus(tiles), m)

                pairs(sp, 0, tiles, tile)
                sp.wait_ge(stored[0], 16 * tiles)
                sp.wait_ge(stored[1], 16 * tiles)

        @block.gpsimd
        def _(pool):
            pool.dma_start(w1_node[:, :], w1[0:F_NODE, :]).then_inc(weights_in, 16)
            pool.dma_start(w1_edge[:, :], w1[F_NODE:F_NODE + F_EDGE, :]).then_inc(weights_in, 16)
            pool.dma_start(w1_global[:, :], w1[F_NODE + F_EDGE:, :]).then_inc(weights_in, 16)
            pool.dma_start(w2_sb[:, :, :], w2.rearrange("(c p) n -> p c n", p=P)).then_inc(weights_in, 16)
            pool.dma_start(global_col[:, :], graph_globals[0:1, :].rearrange("a g -> g a"))\
                .then_inc(weights_in, 16)
            pool.dma_start(b1_col[:, :], b1.rearrange("(c p) -> p c", p=P)).then_inc(weights_in, 16)
            for j in range(2):
                pool.dma_start(b2_rows[:, j, :], bass.AP(tensor=b2.tensor, offset=0,
                                                         ap=[[0, P], [1, F_NODE]])).then_inc(weights_in, 16)
            pool.memset(ones[:, :], 1.0).then_inc(ident_ready, 1)
            pool.wait_ge(ident_ready, 1)
            pool.affine_select(out=ident[:, :], in_=ones[:, :], compare_op=ALU.is_equal, fill=0.0,
                               base=0, pattern=[[-1, P]], channel_multiplier=1).then_inc(ident_ready, 1)
            pool.iota(ramp[:, :], [[1, STEP_WINDOW]], base=0, channel_multiplier=0,
                      allow_small_or_imprecise_dtypes=True).then_inc(consts_ready, 1)
            pool.memset(eps_col[:, :], EPS).then_inc(consts_ready, 1)
            pool.iota(final_node[:, :], [[0, 1]], base=-TILE, channel_multiplier=TILE,
                      allow_small_or_imprecise_dtypes=True).then_inc(consts_ready, 1)
            pool.iota(base_floor[:, :], [[TILE, steps]], base=-TILE, channel_multiplier=0,
                      allow_small_or_imprecise_dtypes=True).then_inc(consts_ready, 1)
            for (g0, ng), (low, high) in zip(QUADS, QUAD_WINDOW):
                pool.memset(low_limit[:, g0:g0 + ng], float(low)).then_inc(consts_ready, 1)
                pool.memset(high_limit[:, g0:g0 + ng], float(high - 1)).then_inc(consts_ready, 1)
            pool.memset(violation[:, :], 0.0).then_inc(consts_ready, 1)
            quarter = agg_cols // 4
            for n in range(4):
                end = agg_cols if n == 3 else (n + 1) * quarter
                pool.memset(agg[:, n * quarter:end], 0.0).then_inc(agg_zeroed, 1)
            pool.memset(zeros[:, :], 0.0).then_inc(agg_zeroed, 1)
            pool.iota(general_ramp[:, :], [[1, GENERAL_BLOCK]], base=0, channel_multiplier=0,
                      allow_small_or_imprecise_dtypes=True).then_inc(agg_zeroed, 1)
            pool.wait_ge(weights_in, 8 * 16)

            def x_plus_b2(k):
                pool.wait_ge(x_in[k.parity], k.half * 16 + 16)
                if not (isinstance(k.i, int) and k.value < 2):
                    pool.wait_ge(out_added, k.plus(-1).value)
                pool.tensor_tensor(xb_buf[k.parity][:, :, :], x_buf[k.parity][:, :, :], b2_rows[:, :, :],
                                   ALU.add).then_inc(xb_ready, 1)

            for k in range(2):
                x_plus_b2(At(k))
            pairs(pool, 2, tiles - 2, x_plus_b2)
            pool.wait_ge(worst_ready, 1)
            pool.partition_all_reduce(worst_all[:, :], worst[:, :], P, bass.bass_isa.ReduceOp.max)\
                .then_inc(worst_shared, 1)
            pool.wait_ge(flag_ready, 1)
            flag = pool.value_load(general_flag[0:1, 0:1], min_val=0, max_val=1)
            with pool.If(flag > 0):
                pairs(pool, tiles, tiles, x_plus_b2)

        @block.scalar
        def _(act):
            def copy_rel(n):
                b, h = divmod(n, 2)
                act.wait_ge(rel_turned, n + 1)
                rows = min(P, n_groups - b * P)
                dest = rel[:, b * P * EDGES_PER_ROW:(b * P + rows) * EDGES_PER_ROW]\
                    .rearrange("p (g r) -> p r g", r=EDGES_PER_ROW)[:, 3 * h:3 * h + 3, :]
                act.activation(dest, hidden_bank[h][:, 0:3 * P].rearrange("p (r g) -> p r g", r=3)[:, :, 0:rows],
                               ACT.Copy).then_inc(rel_ready, 1)

            def copy_sums(t):
                act.wait_ge(edges_used, 3 * t.value + 3)
                if not (isinstance(t.i, int) and t.value < 2):
                    act.wait_ge(window_ready, t.plus(-1).value)
                act.activation(group_sums[t.parity][:, 0:2 * F_EDGE], group_bank[t.parity][:, 0:2 * F_EDGE],
                               ACT.Copy).then_inc(sums_copied, 1)
                act.activation(group_sums[t.parity][0:96, 2 * F_EDGE:], group_bank[t.parity][0:96, 2 * F_EDGE:3 * F_EDGE],
                               ACT.Copy).then_inc(sums_copied, 1)

            def deviate(k):
                act.wait_ge(moments_ready, 2 * k.value + 2)
                act.activation(deviation[:, :], mean_var[:, :, 1], ACT.Sqrt, bias=eps_col[:, :])\
                    .then_inc(deviation_ready, 1)

            def normalise(k):
                act.wait_ge(shift_ready, k.plus(1).value)
                if not (isinstance(k.i, int) and k.value < 1):
                    act.wait_ge(x_turned, k.value)
                act.activation(normed_x[:, 0, :], x_buf[k.parity][:, 0, :], ACT.Relu,
                               bias=shift[:, 0:1], scale=inverse[:, 0:1])
                act.activation(normed_x[:, 1, :], x_buf[k.parity][:, 1, :], ACT.Relu,
                               bias=shift[:, 1:2], scale=inverse[:, 1:2]).then_inc(normed, 1)

            def copy_turned(k):
                act.wait_ge(x_turned, k.plus(1).value)
                if not (isinstance(k.i, int) and k.value < 1):
                    act.wait_ge(hidden_ready, 2 * k.value)
                act.activation(normed_t[:, :], turned_bank[:, 0:TILE], ACT.Copy).then_inc(turned_copied, 1)

            def relu_hidden(k):
                if not (isinstance(k.i, int) and k.value < 1):
                    act.wait_ge(out_ready, k.value)
                for c in range(2):
                    act.wait_ge(hidden_ready, 2 * k.value + c + 1)
                    act.activation(hidden[:, c, :], hidden_bank[c][:, 0:TILE], ACT.Relu,
                                   bias=hidden_bias[:, c:c + 1]).then_inc(hidden_copied, 1)

            def step(s):
                early = isinstance(s.i, int)
                if not (early and s.value < 1):
                    copy_sums(s.plus(-1))
                if not (early and s.value < LAG):
                    copy_turned(s.plus(-LAG))
                if not (early and (s.value < LAG - 1)):
                    deviate(s.plus(1 - LAG))
                if not (early and s.value < LAG):
                    relu_hidden(s.plus(-LAG))
                if not (early and (s.value < LAG - 1)):
                    normalise(s.plus(1 - LAG))

            act.wait_ge(consts_ready, 11)
            for n in range(2):
                copy_rel(n)
            act.wait_ge(position_turned, 1)
            act.activation(position[:, :], out_bank[:, 0:3 * steps], ACT.Copy).then_inc(position_ready, 1)
            act.wait_ge(bias_summed, 1)
            act.wait_ge(weights_in, 8 * 16)
            for c in range(2):
                act.activation(hidden_bias[:, c:c + 1], turned_bank[:, c:c + 1], ACT.Identity,
                               bias=b1_col[:, c:c + 1]).then_inc(bias_ready, 1)
            for n in range(2, 2 * blocks):
                copy_rel(n)
            act.wait_ge(bias_ready, 2)
            for s in range(LAG + 2):
                step(At(s))
            pairs(act, LAG + 2, steps - 3 - LAG, step)
            step(At(steps - 1))
            copy_sums(At(steps - 1))
            for k in range(tiles - LAG, tiles):
                copy_turned(At(k))
                if k + 1 < tiles:
                    deviate(At(k + 1))
                relu_hidden(At(k))
                if k + 1 < tiles:
                    normalise(At(k + 1))
            act.wait_ge(flag_ready, 1)
            flag = act.value_load(general_flag[0:1, 0:1], min_val=0, max_val=1)
            with act.If(flag > 0):
                def tile(k):
                    deviate(k)
                    normalise(k)
                    copy_turned(k)
                    relu_hidden(k)

                pairs(act, tiles, tiles, tile)

        @block.vector
        def _(dve):
            chain = [0]

            def link(ins):
                chain[0] += 1
                ins.then_inc(setup_chain, 1)
                dve.wait_ge(setup_chain, chain[0])

            def relative(b):
                rows = min(P, n_groups - b * P)
                n = (b * P < n_groups - GROUPS) + 3 * (b == blocks - 1)
                dve.wait_ge(dst_in[b], 16 * n)
                dve.tensor_scalar(rel_rows[0:rows, b, :], dst_rows[0:rows, b, 0:group_edges],
                                  dst_rows[0:rows, b, 0:1], None, ALU.subtract).then_inc(rel_rows_ready, 1)

            def check_sorted(b):
                rows = min(P, n_groups - b * P)
                link(dve.tensor_tensor_reduce(
                    out=order_scrap[0:rows, :], in0=dst_rows[0:rows, b, 0:group_edges],
                    in1=dst_rows[0:rows, b, 1:], scale=1.0, scalar=-1.0, op0=ALU.subtract, op1=ALU.max,
                    accum_out=violation[0:rows, b:b + 1]))

            def tables():
                dve.wait_ge(tables_in, 6 * 16)
                dve.wait_ge(consts_ready, 11)
                link(dve.memset(first_f[:, GROUPS:], 0.0))
                link(dve.tensor_copy(first_f[:, 0:GROUPS], first_i[:, :]))
                link(dve.tensor_copy(last_f[:, :], last_i[:, :]))
                link(dve.tensor_scalar(first_rel[:, :], first_f[:, :], first_f[:, 0:1], None, ALU.subtract))
                link(dve.tensor_scalar(last_rel[:, :], last_f[:, :], first_f[:, 0:1], None, ALU.subtract))
                link(dve.tensor_tensor(step_base_f[:, :], step_base_i[:, :], base_floor[:, :], ALU.max))
                link(dve.tensor_scalar(step_base[:, :], step_base_f[:, :], 0.0, float(nodes - 1), ALU.max, ALU.min))
                padded = first_rel[:, :].unsqueeze(2).to_broadcast([steps, 12, WINDOW])
                steps_ramp = ramp[0:steps, 0:WINDOW].unsqueeze(1).to_broadcast([steps, 12, WINDOW])
                dve.tensor_tensor(spread[:, :, :, :].rearrange("s q j w -> s (q j) w"), padded, steps_ramp,
                                  ALU.add).then_inc(spread_ready, 1)

            def check_windows():
                link(dve.tensor_tensor(tests[:, 0, :], last_rel[:, :], first_rel[:, 0:GROUPS], ALU.subtract))
                link(dve.tensor_scalar(tests[:, 0, :], tests[:, 0, :], float(1 - WINDOW), None, ALU.add))
                link(dve.tensor_tensor(tests[:, 1, :], low_limit[:, :], first_rel[:, 0:GROUPS], ALU.subtract))
                link(dve.tensor_tensor(tests[:, 2, :], last_rel[:, :], high_limit[:, :], ALU.subtract))
                link(dve.tensor_scalar(tests[:, 3, :], first_f[:, 0:GROUPS], final_node[:, 0:1], -1.0,
                                       ALU.subtract, ALU.mult))
                link(dve.tensor_scalar(tests[:, 4, :], last_f[:, :], float(1 - nodes), None, ALU.add))
                link(dve.tensor_scalar(tests[:, 5, :], first_f[:, 0:GROUPS], -1.0, None, ALU.mult))
                link(dve.tensor_reduce(violation[0:steps, blocks:], tests[:, :, :].rearrange("s a g -> s (a g)"),
                                       AX.X, ALU.max))
                dve.tensor_reduce(worst[:, :], violation[:, :], AX.X, ALU.max).then_inc(worst_ready, 1)

            def make_onehot(t, q):
                g0, ng = QUADS[q]
                if not (isinstance(t.i, int) and t.value < 2):
                    dve.wait_ge(edges_used, 3 * t.plus(-2).value + q + 1)
                cols = ng * EDGES_PER_ROW
                c0 = g0 * EDGES_PER_ROW
                dve.tensor_tensor(
                    onehot[t.parity][:, c0:c0 + cols, :],
                    rel[:, bass.ds(t.value * STEP_COLS + c0, cols)].unsqueeze(2).to_broadcast([P, cols, WINDOW]),
                    ramp[:, 0:WINDOW].unsqueeze(1).to_broadcast([P, cols, WINDOW]),
                    ALU.is_equal).then_inc(onehot_ready, 1)

            def make_placing(t):
                if not (isinstance(t.i, int) and t.value < 2):
                    dve.wait_ge(window_ready, t.plus(-1).value)
                for q, (low, high) in enumerate(QUAD_WINDOW):
                    rows = QUADS[q][1] * WINDOW
                    dve.tensor_scalar(placing[t.parity][0:rows, q, 0:high - low], ramp[0:rows, low:high],
                                      position[0:rows, bass.ds(t.value + q * steps, 1)], None,
                                      ALU.is_equal).then_inc(placing_ready, 1)

            def add_window(t):
                base = dve.value_load(step_base[0:1, bass.ds(t.value, 1)], min_val=0, max_val=nodes - 1)
                place = agg[:, bass.ds(base, STEP_WINDOW)]
                dve.wait_ge(window_ready, t.plus(1).value)
                if not (isinstance(t.i, int) and t.value < 1):
                    dve.wait_ge(agg_added, t.value)
                dve.tensor_tensor(place, place, window_bank[t.parity][0:F_EDGE, 0:STEP_WINDOW], ALU.add)\
                    .then_inc(agg_added, 1)

            def moments(k):
                dve.wait_ge(x_in[k.parity], k.half * 16 + 16)
                if not (isinstance(k.i, int) and k.value < 1):
                    dve.wait_ge(shift_ready, k.value)
                for j in range(2):
                    dve.bn_stats(bn6[:, j, :], x_buf[k.parity][:, j, :]).then_inc(moments_halfway, 1)

            def join_moments(k):
                for j in range(2):
                    dve.bn_aggr(mean_var[:, j, :], bn6[:, j, :]).then_inc(moments_ready, 1)

            def invert(k):
                dve.wait_ge(deviation_ready, k.plus(1).value)
                if not (isinstance(k.i, int) and k.value < 1):
                    dve.wait_ge(normed, k.value)
                dve.reciprocal(inverse[:, :], deviation[:, :]).then_inc(inverse_ready, 1)
                dve.wait_ge(inverse_ready, k.plus(1).value)
                dve.scalar_tensor_tensor(out=shift[:, :], in0=mean_var[:, :, 0], scalar=-1.0, in1=inverse[:, :],
                                         op0=ALU.mult, op1=ALU.mult).then_inc(shift_ready, 1)

            def add_out(k):
                dve.wait_ge(out_ready, k.plus(1).value)
                dve.wait_ge(xb_ready, k.plus(1).value)
                if not (isinstance(k.i, int) and k.value < 2):
                    dve.wait_ge(stored[k.parity], k.half * 16)
                dve.tensor_tensor(out_buf[k.parity][:, :, :], out_bank[:, 0:TILE].rearrange("p (j f) -> p j f", j=2),
                                  xb_buf[k.parity][:, :, :], ALU.add).then_inc(out_added, 1)

            def step(s):
                early = isinstance(s.i, int)
                more = not (early and s.value + 1 >= steps)
                if not (early and s.value < LAG + 1):
                    add_out(s.plus(-LAG - 1))
                if more:
                    make_onehot(s.plus(1), 0)
                if not (early and s.value < LAG - 1):
                    moments(s.plus(1 - LAG))
                if not (early and s.value < LAG - 1):
                    dve.wait_ge(moments_halfway, 2 * s.plus(1 - LAG).value + 2)
                if more:
                    make_onehot(s.plus(1), 1)
                if not (early and s.value < LAG - 1):
                    join_moments(s.plus(1 - LAG))
                if not (early and s.value < 1):
                    add_window(s.plus(-1))
                if not (early and s.value < LAG - 1):
                    invert(s.plus(1 - LAG))
                if more:
                    make_onehot(s.plus(1), 2)
                make_placing(s)

            relative(0)
            tables()
            dve.wait_ge(rel_ready, 2)
            for q in range(3):
                make_onehot(At(0), q)
            for b in range(1, blocks):
                relative(b)
            dve.wait_ge(rel_ready, 2 * blocks)
            last_cols = (steps - 1) * STEP_COLS
            link(dve.memset(rel[:, last_cols:last_cols + EDGES_PER_ROW], -1.0))
            link(dve.memset(rel[0:masked_row, last_cols + EDGES_PER_ROW:last_cols + 2 * EDGES_PER_ROW], -1.0))
            dve.wait_ge(agg_zeroed, 6)
            dve.wait_ge(position_ready, 1)
            for s in range(LAG + 3):
                step(At(s))
            pairs(dve, LAG + 3, steps - 4 - LAG, step)
            step(At(steps - 1))
            add_out(At(tiles - LAG - 1))
            add_window(At(steps - 1))
            for k in range(tiles - LAG, tiles):
                if k + 1 < tiles:
                    moments(At(k + 1))
                    dve.wait_ge(moments_halfway, 2 * (k + 1) + 2)
                    join_moments(At(k + 1))
                    invert(At(k + 1))
                if k == tiles - LAG:
                    for b in range(blocks):
                        check_sorted(b)
                    check_windows()
                add_out(At(k))
            dve.wait_ge(worst_shared, 1)
            dve.tensor_scalar(general_flag[:, :], worst_all[0:1, :], 0.0, None, ALU.is_gt).then_inc(flag_ready, 1)

            dve.wait_ge(flag_ready, 1)
            flag = dve.value_load(general_flag[0:1, 0:1], min_val=0, max_val=1)
            with dve.If(flag > 0):
                dve.sem_inc(general_staged, 1)
                dve.sem_inc(general_added, 1)

                def chunk(b, c, last):
                    n = b * steps + c
                    dve.wait_ge(general_dst_in, n * 16 + 16)
                    dve.wait_ge(general_staged, n * (2 * GROUPS) + 1)
                    dve.tensor_copy(general_rel[:, :], general_dst[:, :, :].rearrange("p g r -> p (g r)"))\
                        .then_inc(general_rel_chain, 1)
                    dve.wait_ge(general_rel_chain, n * 3 + 1)
                    if last:
                        dve.memset(general_rel[:, 0:EDGES_PER_ROW], -1.0).then_inc(general_rel_chain, 1)
                        dve.memset(general_rel[0:masked_row, EDGES_PER_ROW:2 * EDGES_PER_ROW], -1.0)\
                            .then_inc(general_rel_chain, 1)
                    else:
                        dve.sem_inc(general_rel_chain, 2)
                    with dve.Fori(0, GROUPS) as g:
                        dve.wait_ge(general_edges_in, n * 16 + 16)
                        dve.wait_ge(general_used, n * GROUPS + g + 1)
                        dve.tensor_copy(general_edges[:, :], edge_buf[0][:, :, :].rearrange("p g d -> p (g d)")
                                        [:, bass.ds(g * ROW, ROW)]).then_inc(general_staged, 1)
                        dve.wait_ge(general_rel_chain, n * 3 + 3)
                        dve.wait_ge(general_added, 2 * b + 1)
                        dve.tensor_tensor(
                            general_onehot[:, :, :],
                            general_rel[:, bass.ds(g * EDGES_PER_ROW, EDGES_PER_ROW)].unsqueeze(2)
                            .to_broadcast([P, EDGES_PER_ROW, GENERAL_BLOCK]),
                            general_ramp[:, :].unsqueeze(1).to_broadcast([P, EDGES_PER_ROW, GENERAL_BLOCK]),
                            ALU.is_equal).then_inc(general_staged, 1)

                with dve.Fori(0, blocks_g) as b:
                    with dve.Fori(0, steps - 1) as c:
                        chunk(b, c, False)
                    chunk(b, steps - 1, True)
                    dve.wait_ge(general_summed, b + 1)
                    dve.tensor_copy(agg[:, bass.ds(b * GENERAL_BLOCK, GENERAL_BLOCK)],
                                    window_bank[0][0:F_EDGE, 0:GENERAL_BLOCK]).then_inc(general_added, 1)
                    dve.wait_ge(general_added, 2 * b + 2)
                    dve.tensor_scalar(general_ramp[:, :], general_ramp[:, :], float(GENERAL_BLOCK), None,
                                      ALU.add).then_inc(general_added, 1)

                def tile(k):
                    moments(k)
                    dve.wait_ge(moments_halfway, 2 * k.value + 2)
                    dve.tensor_copy(general_rel[:, 0:1], eps_col[:, :])
                    join_moments(k)
                    invert(k)
                    add_out(k)

                pairs(dve, tiles, tiles, tile)

        @block.tensor
        def _(pe):
            def turn_rel(n):
                b, h = divmod(n, 2)
                rows = min(P, n_groups - b * P)
                pe.wait_ge(rel_rows_ready, b + 1)
                if n >= 2:
                    pe.wait_ge(rel_ready, n - 1)
                for r in range(3):
                    last = pe.transpose(
                        hidden_bank[h][:, r * P:r * P + rows],
                        rel_rows[0:rows, b, :].rearrange("g (p r) -> g r p", r=EDGES_PER_ROW)[:, 3 * h + r, :],
                        ident[0:rows, 0:rows])
                last.then_inc(rel_turned, 1)

            def sum_quad(t, q):
                g0, ng = QUADS[q]
                p = t.parity
                pe.wait_ge(edges_in[p][q], t.half * 16 + 16)
                pe.wait_ge(onehot_ready, 3 * t.value + q + 1)
                if q == 0 and not (isinstance(t.i, int) and t.value < 2):
                    pe.wait_ge(sums_copied, 2 * t.plus(-1).value)
                for pair in (range(0, 2), range(2, ng)):
                    for r in range(EDGES_PER_ROW):
                        for j in pair:
                            last = pe.matmul(
                                group_bank[p][WINDOW * j:WINDOW * (j + 1), q * F_EDGE:(q + 1) * F_EDGE],
                                onehot[p][:, (g0 + j) * EDGES_PER_ROW + r, :],
                                edge_buf[p][:, g0 + j, r * F_EDGE:(r + 1) * F_EDGE],
                                start=(r == 0), stop=(r == EDGES_PER_ROW - 1))
                last.then_inc(edges_used, 1)

            def place_sums(t):
                p = t.parity
                pe.wait_ge(sums_copied, 2 * t.value + 2)
                pe.wait_ge(placing_ready, 3 * t.value + 3)
                if not (isinstance(t.i, int) and t.value < 2):
                    pe.wait_ge(agg_added, t.plus(-1).value)
                for q, (low, high) in enumerate(QUAD_WINDOW):
                    rows = QUADS[q][1] * WINDOW
                    last = pe.matmul(window_bank[p][0:F_EDGE, low:high],
                                     group_sums[p][0:rows, q * F_EDGE:(q + 1) * F_EDGE],
                                     placing[p][0:rows, q, 0:high - low],
                                     start=(q == 0), stop=(q == 2), skip_group_check=True)
                last.then_inc(window_ready, 1)

            def turn_x(k):
                pe.wait_ge(normed, k.plus(1).value)
                if not (isinstance(k.i, int) and k.value < 1):
                    pe.wait_ge(turned_copied, k.value)
                for j in range(2):
                    last = pe.transpose(turned_bank[:, j * P:(j + 1) * P], normed_x[:, j, :], ident[:, :])
                last.then_inc(x_turned, 1)

            def first_layer(k, m, sums):
                pe.wait_ge(turned_copied, k.plus(1).value)
                pe.wait_ge(*sums)
                if not (isinstance(k.i, int) and k.value < 1):
                    pe.wait_ge(hidden_copied, 2 * k.value)
                tile_sums = agg[:, bass.ds(tile_node0(m), TILE)].rearrange("f (p j) -> f j p", j=2)
                for c in range(2):
                    units = slice(c * P, (c + 1) * P)
                    pe.matmul(hidden_bank[c][:, 0:TILE], w1_node[:, units], normed_t[:, :], start=True, stop=False)
                    pe.matmul(hidden_bank[c][:, 0:TILE].rearrange("u (j p) -> u j p", j=2), w1_edge[:, units],
                              tile_sums, start=False, stop=True).then_inc(hidden_ready, 1)

            def second_layer(k):
                pe.wait_ge(hidden_copied, 2 * k.value + 2)
                if not (isinstance(k.i, int) and k.value < 1):
                    pe.wait_ge(out_added, k.value)
                for j in range(2):
                    for c in range(2):
                        last = pe.matmul(out_bank[:, j * P:(j + 1) * P], hidden[:, c, j * P:(j + 1) * P],
                                         w2_sb[:, c, :], start=(c == 0), stop=(c == 1))
                last.then_inc(out_ready, 1)

            def sums_of(k):
                if isinstance(k.i, int) and k.value + 2 > steps:
                    return agg_added, steps
                return agg_added, k.plus(2).value

            def step(s):
                late = not (isinstance(s.i, int) and s.value < LAG)
                k = s.plus(-LAG)
                sum_quad(s, 0)
                if not (isinstance(s.i, int) and s.value < 1):
                    place_sums(s.plus(-1))
                if late:
                    turn_x(k)
                sum_quad(s, 1)
                if late:
                    first_layer(k, k, sums_of(k))
                sum_quad(s, 2)
                if late:
                    second_layer(k)

            pe.wait_ge(ident_ready, 2)
            for n in range(2):
                turn_rel(n)
            pe.wait_ge(spread_ready, 1)
            for q in range(3):
                last = pe.transpose(out_bank[:, q * steps:(q + 1) * steps],
                                    spread[:, q, :, :].rearrange("s j w -> s (j w)"), ident[0:steps, 0:steps])
            last.then_inc(position_turned, 1)
            pe.wait_ge(weights_in, 8 * 16)
            for c in range(2):
                last = pe.matmul(turned_bank[:, c:c + 1], w1_global[:, c * P:(c + 1) * P], global_col[:, :],
                                 start=True, stop=True)
            last.then_inc(bias_summed, 1)
            for n in range(2, 2 * blocks):
                turn_rel(n)
            pe.wait_ge(rel_ready, 2 * blocks)
            pe.wait_ge(bias_ready, 2)
            pe.wait_ge(position_ready, 1)
            for s in range(LAG + 2):
                step(At(s))
            pairs(pe, LAG + 2, steps - 3 - LAG, step)
            step(At(steps - 1))
            for k in range(tiles - LAG, tiles):
                turn_x(At(k))
                first_layer(At(k), At(k), sums_of(At(k)))
                if k == tiles - LAG:
                    place_sums(At(steps - 1))
                second_layer(At(k))

            pe.wait_ge(flag_ready, 1)
            flag = pe.value_load(general_flag[0:1, 0:1], min_val=0, max_val=1)
            with pe.If(flag > 0):
                pe.sem_inc(general_used, 1)
                bank_g = window_bank[0][0:F_EDGE, 0:GENERAL_BLOCK]

                def chunk(b, c):
                    with pe.Fori(0, GROUPS) as g:
                        n = (b * steps + c) * GROUPS + g
                        pe.wait_ge(general_staged, n * 2 + 3)
                        for r in range(EDGES_PER_ROW):
                            last = pe.matmul(bank_g, general_edges[:, r * F_EDGE:(r + 1) * F_EDGE],
                                             general_onehot[:, r, :], start=False, stop=False)
                        last.then_inc(general_used, 1)

                with pe.Fori(0, blocks_g) as b:
                    pe.wait_ge(general_added, b * 2 + 1)
                    pe.matmul(bank_g, zeros[0:1, 0:F_EDGE], zeros[0:1, :], start=True, stop=False)
                    with pe.Fori(0, steps - 1) as c:
                        chunk(b, c)
                    chunk(b, steps - 1)
                    pe.matmul(bank_g, zeros[0:1, 0:F_EDGE], zeros[0:1, :], start=False, stop=True)\
                        .then_inc(general_summed, 1)

                def tile(m):
                    k = m.plus(tiles)
                    turn_x(k)
                    first_layer(k, m, (general_added, 2 * blocks_g + 1))
                    second_layer(k)

                pairs(pe, 0, tiles, tile)


_INS = ["x", "dst", "edge_attr_48", "L0_gnn_graph_globals", "L0_gnn_W1", "L0_gnn_b1", "L0_gnn_W2", "L0_gnn_b2"]


def kernel(**inputs):
    import numpy as _np
    import concourse.bacc as _bacc
    from concourse import mybir as _mybir
    from concourse.bass_utils import run_bass_kernel_spmd as _run

    nc = _bacc.Bacc("TRN2", target_bir_lowering=False, num_devices=1)
    arrays, args = {}, []
    for name in _INS:
        a = _np.ascontiguousarray(inputs[name])
        arrays[f"in_{name}"] = a
        args.append(nc.dram_tensor(f"in_{name}", a.shape, _mybir.dt.from_np(a.dtype), kind="ExternalInput").ap())
    shape = arrays["in_x"].shape
    args.append(nc.dram_tensor("out_0", shape, _mybir.dt.from_np(_np.dtype("float32")), kind="ExternalOutput").ap())
    gnn_kernel(nc, *args)
    return _run(nc, [arrays], core_ids=[0]).results[0]["out_0"]
```

```python
import concourse.bass as bass
from concourse import mybir
from contextlib import ExitStack

P = 128
EDGES_PER_ROW = 6
WINDOW = 32
GROUPS = 11
QUADS = ((0, 4), (4, 4), (8, 3))
QUAD_WINDOW = ((0, 104), (84, 196), (176, 276))
STEP_WINDOW = 276
TILE = 256
LAG = 3
F_NODE, F_EDGE, F_GLOBAL, HIDDEN = 128, 48, 64, 256
STACK, STACK_LOW = 112, 64
GENERAL_BLOCK = 512
EPS = 1e-5


class At:

    def __init__(self, c, i=0):
        self.c, self.i = c, i

    @property
    def value(self):
        return self.i * 2 + self.c if not isinstance(self.i, int) else self.c + 2 * self.i

    @property
    def parity(self):
        return self.c % 2

    @property
    def half(self):
        return self.i + self.c // 2

    def plus(self, n):
        return At(self.c + n, self.i)


def gnn_kernel(nc, x, dst, edges, graph_globals, w1, b1, w2, b2, out):
    fp32, fp32r, i32 = mybir.dt.float32, mybir.dt.float32r, mybir.dt.int32
    ALU = mybir.AluOpType
    ACT = mybir.ActivationFunctionType
    AX = mybir.AxisListType

    nodes, n_edges = x.shape[0], edges.shape[0]
    group_edges = P * EDGES_PER_ROW
    step_edges = group_edges * GROUPS
    steps = -(-n_edges // step_edges)
    tiles = -(-nodes // TILE)
    last_edge0 = n_edges - step_edges
    repeated = steps * step_edges - n_edges
    last_node0 = nodes - TILE
    fresh_row = (tiles * TILE - nodes) // 2
    masked_row = (repeated - group_edges) // EDGES_PER_ROW
    assert group_edges < repeated < 2 * group_edges and repeated % EDGES_PER_ROW == 0
    assert (tiles * TILE - nodes) % 2 == 0 and steps == tiles and steps % 2 == 1 and steps >= 7
    ROW = EDGES_PER_ROW * F_EDGE
    LOW = 3 * F_EDGE
    SPLIT_COLS = 2 * LOW + F_EDGE
    STEP_COLS = GROUPS * EDGES_PER_ROW
    n_groups = steps * GROUPS
    blocks = -(-n_groups // P)
    blocks_g = -(-nodes // GENERAL_BLOCK)
    agg_cols = -(-max(blocks_g * GENERAL_BLOCK, nodes + STEP_WINDOW) // 4) * 4
    quarter = agg_cols // 4

    ctx = ExitStack()
    with ctx:
        def sb(name, shape, dt=fp32):
            return ctx.enter_context(nc.sbuf_tensor(name, shape, dt))

        def bank(name):
            return ctx.enter_context(nc.psum_tensor(name, [P, 512], fp32))

        def sem(name):
            return ctx.enter_context(nc.semaphore(name))

        edge_buf = [sb(f"edge_buf{p}", [P, GROUPS, ROW]) for p in range(2)]
        onehot = [sb(f"onehot{p}", [P, STEP_COLS, WINDOW]) for p in range(2)]
        group_sums = [sb(f"group_sums{p}", [P, 3 * F_EDGE]) for p in range(2)]
        split_sums = [sb(f"split_sums{p}", [P, SPLIT_COLS], fp32r) for p in range(2)]
        placing = [sb(f"placing{p}", [P, 3, 112], fp32r) for p in range(2)]
        agg = sb("agg", [F_EDGE, agg_cols])
        dst_rows = sb("dst_rows", [P, blocks, group_edges + 1], i32)
        rel_rows = sb("rel_rows", [P, blocks, group_edges])
        order_scrap = sb("order_scrap", [P, group_edges])
        rel = sb("rel", [P, blocks * P * EDGES_PER_ROW])
        first_i = sb("first_i", [steps, GROUPS], i32)
        last_i = sb("last_i", [steps, GROUPS], i32)
        first_f = sb("first_f", [steps, GROUPS + 1])
        last_f = sb("last_f", [steps, GROUPS])
        first_rel = sb("first_rel", [steps, GROUPS + 1])
        last_rel = sb("last_rel", [steps, GROUPS])
        tests = sb("tests", [steps, 6, GROUPS])
        low_limit = sb("low_limit", [steps, GROUPS])
        high_limit = sb("high_limit", [steps, GROUPS])
        final_node = sb("final_node", [steps, 1])
        spread = sb("spread", [steps, 3, 4, WINDOW])
        position = sb("position", [P, 3 * steps])
        step_base_i = sb("step_base_i", [1, steps], i32)
        step_base_f = sb("step_base_f", [1, steps])
        base_floor = sb("base_floor", [1, steps])
        step_base = sb("step_base", [1, steps], i32)
        violation = sb("violation", [P, blocks + 1])
        worst = sb("worst", [P, 1])
        worst_all = sb("worst_all", [P, 1])
        general_flag = sb("general_flag", [1, 1], i32)
        ramp = sb("ramp", [P, STEP_WINDOW])
        ones = sb("ones", [P, P])
        ident = sb("ident", [P, P])
        zeros = sb("zeros", [F_EDGE, GENERAL_BLOCK])
        w1_node = sb("w1_node", [F_NODE, HIDDEN])
        w1_edge = sb("w1_edge", [STACK, HIDDEN])
        w1_high = sb("w1_high", [STACK, HIDDEN], fp32r)
        w1_low = sb("w1_low", [STACK, HIDDEN], fp32r)
        tile_sums = sb("tile_sums", [STACK, TILE], fp32r)
        w1_global = sb("w1_global", [F_GLOBAL, HIDDEN])
        w2_sb = sb("w2_sb", [P, 2, F_NODE])
        global_col = sb("global_col", [F_GLOBAL, 1])
        b1_col = sb("b1_col", [P, 2])
        hidden_bias = sb("hidden_bias", [P, 2])
        b2_rows = sb("b2_rows", [P, 2, F_NODE])
        eps_col = sb("eps_col", [P, 1])
        x_buf = [sb(f"x_buf{p}", [P, 2, F_NODE]) for p in range(2)]
        xb_buf = [sb(f"xb_buf{p}", [P, 2, F_NODE]) for p in range(2)]
        out_buf = [sb(f"out_buf{p}", [P, 2, F_NODE]) for p in range(2)]
        bn6 = sb("bn6", [P, 2, 6])
        mean_var = sb("mean_var", [P, 2, 2])
        deviation = sb("deviation", [P, 2])
        inverse = sb("inverse", [P, 2])
        shift = sb("shift", [P, 2])
        normed_x = sb("normed_x", [P, 2, F_NODE])
        normed_t = sb("normed_t", [P, TILE])
        hidden = sb("hidden", [P, 2, TILE])
        mlp_out = sb("mlp_out", [P, 2, F_NODE])
        general_edges = sb("general_edges", [P, ROW])
        general_dst = sb("general_dst", [P, GROUPS, EDGES_PER_ROW], i32)
        general_rel = sb("general_rel", [P, STEP_COLS])
        general_onehot = sb("general_onehot", [P, EDGES_PER_ROW, GENERAL_BLOCK])
        general_ramp = sb("general_ramp", [P, GENERAL_BLOCK])

        group_bank = [bank(f"group_bank{p}") for p in range(2)]
        window_bank = [bank(f"window_bank{p}") for p in range(2)]
        turned_bank, out_bank = bank("turned_bank"), bank("out_bank")
        hidden_bank = [bank(f"hidden_bank{c}") for c in range(2)]

        dst_in = [sem(f"dst_in{b}") for b in range(blocks)]
        tables_in = sem("tables_in")
        weights_in = sem("weights_in")
        edges_in = [[sem(f"edges_in{p}{q}") for q in range(3)] for p in range(2)]
        x_in = [sem(f"x_in{p}") for p in range(2)]
        stored = [sem(f"stored{p}") for p in range(2)]
        consts_ready = sem("consts_ready")
        eps_ready = sem("eps_ready")
        ident_ready = sem("ident_ready")
        zeros_ready = sem("zeros_ready")
        agg_zeroed = sem("agg_zeroed")
        rel_rows_ready = sem("rel_rows_ready")
        rel_turned = sem("rel_turned")
        rel_ready = sem("rel_ready")
        tables_ready = sem("tables_ready")
        spread_ready = sem("spread_ready")
        position_turned = sem("position_turned")
        position_ready = sem("position_ready")
        bias_summed = sem("bias_summed")
        bias_ready = sem("bias_ready")
        setup_chain = sem("setup_chain")
        setup_scalar = sem("setup_scalar")
        onehot_ready = sem("onehot_ready")
        edges_used = sem("edges_used")
        sums_copied = sem("sums_copied")
        placing_ready = sem("placing_ready")
        window_ready = sem("window_ready")
        agg_added = sem("agg_added")
        moments_halfway = sem("moments_halfway")
        moments_ready = sem("moments_ready")
        deviation_ready = sem("deviation_ready")
        inverse_ready = sem("inverse_ready")
        shift_ready = sem("shift_ready")
        normed = sem("normed")
        x_turned = sem("x_turned")
        turned_copied = sem("turned_copied")
        hidden_ready = sem("hidden_ready")
        hidden_copied = sem("hidden_copied")
        out_ready = sem("out_ready")
        xb_ready = sem("xb_ready")
        out_copied = sem("out_copied")
        out_added = sem("out_added")
        stacks_zeroed = sem("stacks_zeroed")
        w1_high_ready = sem("w1_high_ready")
        w1_split = sem("w1_split")
        sums_split = sem("sums_split")
        tile_high_ready = sem("tile_high_ready")
        tile_low_ready = sem("tile_low_ready")
        worst_ready = sem("worst_ready")
        worst_shared = sem("worst_shared")
        flag_ready = sem("flag_ready")
        general_ramp_ready = sem("general_ramp_ready")
        general_edges_in = sem("general_edges_in")
        general_dst_in = sem("general_dst_in")
        general_rel_chain = sem("general_rel_chain")
        general_rel_ready = sem("general_rel_ready")
        general_staged = sem("general_staged")
        general_used = sem("general_used")
        general_summed = sem("general_summed")
        general_added = sem("general_added")

        edge_view = edges.rearrange("e d -> (e d)")

        def tile_node0(m):
            if isinstance(m.i, int) and m.value == tiles - 1:
                return last_node0
            return m.value * TILE

        def step_edge0(t):
            if isinstance(t.i, int) and t.value == steps - 1:
                return last_edge0
            return t.value * step_edges

        def pairs(eng, first, count, body):
            if count >= 2:
                with eng.Fori(0, count // 2) as i:
                    body(At(first, i))
                    body(At(first + 1, i))
            if count % 2:
                body(At(first + count - 1))

        ctx.enter_context(nc.allow_non_contiguous_dma(reason="a few small columns of dst, biases"))
        def sums_of(k):
            if isinstance(k.i, int) and k.value + 2 > steps:
                return agg_added, steps
            return agg_added, k.plus(2).value

        def setup_batches(s):
            return range(min(2 + 3 * s, 2 * blocks), min(5 + 3 * s, 2 * blocks))

        block = ctx.enter_context(nc.Block())

        @block.sync
        def _(sp):
            def load_dst(b):
                first = b * P * group_edges
                rows = min(P, n_groups - GROUPS - b * P)
                if rows > 0:
                    sp.dma_start(dst_rows[0:rows, b, :], bass.AP(
                        tensor=dst.tensor, offset=first, ap=[[group_edges, rows], [1, group_edges + 1]]))\
                        .then_inc(dst_in[b], 16)
                if b == blocks - 1:
                    rows = max(rows, 0)
                    sp.dma_start(dst_rows[rows:rows + GROUPS - 1, b, :], bass.AP(
                        tensor=dst.tensor, offset=last_edge0,
                        ap=[[group_edges, GROUPS - 1], [1, group_edges + 1]])).then_inc(dst_in[b], 16)
                    rows += GROUPS - 1
                    sp.dma_start(dst_rows[rows:rows + 1, b, 0:group_edges],
                                 dst[n_edges - group_edges:].rearrange("(g e) -> g e", g=1))\
                        .then_inc(dst_in[b], 16)
                    sp.dma_start(dst_rows[rows:rows + 1, b, group_edges:],
                                 dst[n_edges - 1:].rearrange("(g e) -> g e", e=1)).then_inc(dst_in[b], 16)

            def load_edges(t):
                e0 = step_edge0(t)
                for q, (g0, ng) in enumerate(QUADS):
                    if not (isinstance(t.i, int) and t.value < 2):
                        sp.wait_ge(edges_used, 3 * t.plus(-2).value + q + 1)
                    n = ng * group_edges * F_EDGE
                    src = edge_view[bass.ds((e0 + g0 * group_edges) * F_EDGE, n)]
                    sp.dma_start(edge_buf[t.parity][:, g0:g0 + ng, :],
                                 src.rearrange("(g p d) -> p g d", g=ng, p=P))\
                      .then_inc(edges_in[t.parity][q], 16)

            def load_x(k, m):
                if not (isinstance(k.i, int) and k.value < 2):
                    sp.wait_ge(normed, k.plus(-1).value)
                    sp.wait_ge(xb_ready, k.plus(-1).value)
                sp.dma_start(x_buf[k.parity][:, :, :], x[bass.ds(tile_node0(m), TILE), :]
                             .rearrange("(p j) f -> p j f", j=2)).then_inc(x_in[k.parity], 16)

            def store(k, m):
                sp.wait_ge(out_added, k.plus(1).value)
                row = fresh_row if isinstance(m.i, int) and m.value == tiles - 1 else 0
                first = tile_node0(m) + 2 * row
                sp.dma_start(out[bass.ds(first, TILE - 2 * row), :].rearrange("(p j) f -> p j f", j=2),
                             out_buf[k.parity][row:, :, :]).then_inc(stored[k.parity], 16)

            def column(first, rows, stride, cols, col_stride):
                return bass.AP(tensor=dst.tensor, offset=first, ap=[[stride, rows], [col_stride, cols]])

            load_dst(0)
            load_edges(At(0))
            for table, first in ((first_i, 0), (last_i, group_edges - 1)):
                sp.dma_start(table[0:steps - 1, :], column(first, steps - 1, step_edges, GROUPS, group_edges))\
                  .then_inc(tables_in, 16)
                sp.dma_start(table[steps - 1:steps, :], column(last_edge0 + first, 1, 1, GROUPS, group_edges))\
                  .then_inc(tables_in, 16)
            sp.dma_start(step_base_i[0:1, 0:steps - 1], column(0, 1, 1, steps - 1, step_edges))\
              .then_inc(tables_in, 16)
            sp.dma_start(step_base_i[0:1, steps - 1:], column(last_edge0, 1, 1, 1, 1)).then_inc(tables_in, 16)
            for b in range(1, min(2, blocks)):
                load_dst(b)
            load_edges(At(1))
            for b in range(2, blocks):
                load_dst(b)
            load_x(At(0), At(0))
            load_x(At(1), At(1))

            def step(s):
                if not (isinstance(s.i, int) and s.value < 4):
                    store(s.plus(-4), s.plus(-4))
                if not (isinstance(s.i, int) and (s.value < 3 or s.value - 1 >= tiles)):
                    load_x(s.plus(-1), s.plus(-1))
                if not (isinstance(s.i, int) and s.value + 2 >= steps):
                    load_edges(s.plus(2))

            for s in range(4):
                step(At(s))
            pairs(sp, 4, steps - 7, step)
            for s in range(steps - 3, tiles + 4):
                step(At(s))
            sp.wait_ge(stored[0], 16 * ((tiles + 1) // 2))
            sp.wait_ge(stored[1], 16 * (tiles // 2))

            sp.wait_ge(flag_ready, 1)
            flag = sp.value_load(general_flag[0:1, 0:1], min_val=0, max_val=1)
            with sp.If(flag > 0):
                def load_chunk(b, c, edge0):
                    n = b * steps + c
                    sp.wait_ge(general_used, n * GROUPS + 1)
                    src = edge_view[bass.ds(edge0 * F_EDGE, step_edges * F_EDGE)]
                    sp.dma_start(edge_buf[0][:, :, :], src.rearrange("(g p d) -> p g d", g=GROUPS, p=P))\
                      .then_inc(general_edges_in, 16)
                    sp.dma_start(general_dst[:, :, :], dst[bass.ds(edge0, step_edges)]
                                 .rearrange("(g p r) -> p g r", g=GROUPS, p=P)).then_inc(general_dst_in, 16)

                with sp.Fori(0, blocks_g) as b:
                    with sp.Fori(0, steps - 1) as c:
                        load_chunk(b, c, c * step_edges)
                    load_chunk(b, steps - 1, last_edge0)

                def tile(m):
                    load_x(m.plus(tiles), m)
                    store(m.plus(tiles), m)

                pairs(sp, 0, tiles, tile)
                sp.wait_ge(stored[0], 16 * tiles)
                sp.wait_ge(stored[1], 16 * tiles)

        @block.gpsimd
        def _(pool):
            pool.memset(ones[:, :], 1.0).then_inc(ident_ready, 1)
            pool.wait_ge(ident_ready, 1)
            pool.affine_select(out=ident[:, :], in_=ones[:, :], compare_op=ALU.is_equal, fill=0.0,
                               base=0, pattern=[[-1, P]], channel_multiplier=1).then_inc(ident_ready, 1)
            pool.memset(eps_col[:, :], EPS).then_inc(eps_ready, 1)
            pool.iota(ramp[:, :], [[1, STEP_WINDOW]], base=0, channel_multiplier=0,
                      allow_small_or_imprecise_dtypes=True).then_inc(consts_ready, 1)
            pool.iota(final_node[:, :], [[0, 1]], base=-TILE, channel_multiplier=TILE,
                      allow_small_or_imprecise_dtypes=True).then_inc(consts_ready, 1)
            pool.iota(base_floor[:, :], [[TILE, steps]], base=-TILE, channel_multiplier=0,
                      allow_small_or_imprecise_dtypes=True).then_inc(consts_ready, 1)
            for (g0, ng), (low, high) in zip(QUADS, QUAD_WINDOW):
                pool.memset(low_limit[:, g0:g0 + ng], float(low)).then_inc(consts_ready, 1)
                pool.memset(high_limit[:, g0:g0 + ng], float(high - 1)).then_inc(consts_ready, 1)
            pool.memset(violation[:, :], 0.0).then_inc(consts_ready, 1)
            pool.memset(zeros[:, :], 0.0).then_inc(zeros_ready, 1)
            pool.memset(w1_edge[:, :], 0.0).then_inc(stacks_zeroed, 1)
            pool.memset(tile_sums[:, :].bitcast(fp32), 0.0).then_inc(stacks_zeroed, 1)
            for p in range(2):
                pool.memset(group_sums[p][:, :], 0.0).then_inc(stacks_zeroed, 1)
                pool.memset(split_sums[p][:, :].bitcast(fp32), 0.0).then_inc(stacks_zeroed, 1)
            for n in (0, 1):
                pool.memset(agg[:, n * quarter:(n + 1) * quarter], 0.0).then_inc(agg_zeroed, 1)
            pool.dma_start(w1_node[:, :], w1[0:F_NODE, :]).then_inc(weights_in, 16)
            pool.wait_ge(stacks_zeroed, 1)
            for row in (0, STACK_LOW):
                pool.dma_start(w1_edge[row:row + F_EDGE, :], w1[F_NODE:F_NODE + F_EDGE, :])\
                    .then_inc(weights_in, 16)
            pool.dma_start(w1_global[:, :], w1[F_NODE + F_EDGE:, :]).then_inc(weights_in, 16)
            pool.dma_start(w2_sb[:, :, :], w2.rearrange("(c p) n -> p c n", p=P)).then_inc(weights_in, 16)
            pool.dma_start(global_col[:, :], graph_globals[0:1, :].rearrange("a g -> g a")).then_inc(weights_in, 16)
            pool.dma_start(b1_col[:, :], b1.rearrange("(c p) -> p c", p=P)).then_inc(weights_in, 16)
            for j in range(2):
                pool.dma_start(b2_rows[:, j, :], bass.AP(tensor=b2.tensor, offset=0, ap=[[0, P], [1, F_NODE]]))\
                    .then_inc(weights_in, 16)
            pool.iota(general_ramp[:, :], [[1, GENERAL_BLOCK]], base=0, channel_multiplier=0,
                      allow_small_or_imprecise_dtypes=True).then_inc(general_ramp_ready, 1)

            def x_plus_b2(k):
                pool.wait_ge(x_in[k.parity], k.half * 16 + 16)
                if not (isinstance(k.i, int) and k.value < 2):
                    pool.wait_ge(out_added, k.plus(-1).value)
                pool.tensor_tensor(xb_buf[k.parity][:, :, :], x_buf[k.parity][:, :, :], b2_rows[:, :, :],
                                   ALU.add).then_inc(xb_ready, 1)

            def split_low(t):
                if isinstance(t.i, int) and t.value == 0:
                    pool.wait_ge(stacks_zeroed, 6)
                pool.wait_ge(sums_copied, 4 * t.value + 4)
                p = t.parity
                pool.tensor_tensor(split_sums[p][:, LOW:2 * LOW], group_sums[p][:, :],
                                   split_sums[p][:, 0:LOW].bitcast(fp32), ALU.subtract).then_inc(sums_split, 1)

            def add_out(k):
                pool.wait_ge(out_copied, k.plus(1).value)
                pool.wait_ge(xb_ready, k.plus(1).value)
                if not (isinstance(k.i, int) and k.value < 2):
                    pool.wait_ge(stored[k.parity], k.half * 16)
                pool.tensor_tensor(out_buf[k.parity][:, :, :], mlp_out[:, :, :], xb_buf[k.parity][:, :, :],
                                   ALU.add).then_inc(out_added, 1)

            def step(s):
                early = isinstance(s.i, int)
                if not (early and not 1 <= s.value <= steps):
                    split_low(s.plus(-1))
                if not (early and s.value < LAG + 1):
                    add_out(s.plus(-LAG - 1))
                if not (early and not LAG - 1 <= s.value < tiles + LAG - 1):
                    x_plus_b2(s.plus(1 - LAG))

            for s in range(LAG + 3):
                if s == LAG - 1:
                    pool.wait_ge(weights_in, 9 * 16)
                step(At(s))
            pairs(pool, LAG + 3, steps - 4 - LAG, step)
            step(At(steps - 1))
            pool.wait_ge(worst_ready, 1)
            pool.partition_all_reduce(worst_all[:, :], worst[:, :], P, bass.bass_isa.ReduceOp.max)\
                .then_inc(worst_shared, 1)
            for s in range(steps, tiles + LAG + 1):
                step(At(s))
            pool.wait_ge(flag_ready, 1)
            flag = pool.value_load(general_flag[0:1, 0:1], min_val=0, max_val=1)
            with pool.If(flag > 0):
                def tile(k):
                    x_plus_b2(k)
                    add_out(k)

                pairs(pool, tiles, tiles, tile)

        @block.scalar
        def _(act):
            def copy_rel(n):
                b, h = divmod(n, 2)
                act.wait_ge(rel_turned, n + 1)
                rows = min(P, n_groups - b * P)
                dest = rel[:, b * P * EDGES_PER_ROW:(b * P + rows) * EDGES_PER_ROW]\
                    .rearrange("p (g r) -> p r g", r=EDGES_PER_ROW)[:, 3 * h:3 * h + 3, :]
                act.activation(dest, hidden_bank[h][:, 0:3 * P].rearrange("p (r g) -> p r g", r=3)[:, :, 0:rows],
                               ACT.Copy).then_inc(rel_ready, 1)

            def copy_sums(t):
                act.wait_ge(edges_used, 3 * t.value + 3)
                if not (isinstance(t.i, int) and t.value < 2):
                    act.wait_ge(window_ready, t.plus(-1).value)
                for rows, cols in ((P, slice(0, 2 * F_EDGE)), (QUADS[2][1] * WINDOW, slice(2 * F_EDGE, LOW))):
                    for dest in (group_sums, split_sums):
                        act.activation(dest[t.parity][0:rows, cols], group_bank[t.parity][0:rows, cols],
                                       ACT.Copy).then_inc(sums_copied, 1)

            def deviate(k):
                act.wait_ge(moments_ready, 2 * k.value + 2)
                act.activation(deviation[:, :], mean_var[:, :, 1], ACT.Sqrt, bias=eps_col[:, :])\
                    .then_inc(deviation_ready, 1)

            def normalise(k):
                act.wait_ge(shift_ready, k.plus(1).value)
                if not (isinstance(k.i, int) and k.value < 1):
                    act.wait_ge(x_turned, k.value)
                act.activation(normed_x[:, 0, :], x_buf[k.parity][:, 0, :], ACT.Relu,
                               bias=shift[:, 0:1], scale=inverse[:, 0:1])
                act.activation(normed_x[:, 1, :], x_buf[k.parity][:, 1, :], ACT.Relu,
                               bias=shift[:, 1:2], scale=inverse[:, 1:2]).then_inc(normed, 1)

            def copy_turned(k):
                act.wait_ge(x_turned, k.plus(1).value)
                if not (isinstance(k.i, int) and k.value < 1):
                    act.wait_ge(hidden_ready, 2 * k.value)
                act.activation(normed_t[:, :], turned_bank[:, 0:TILE], ACT.Copy).then_inc(turned_copied, 1)

            def tile_high(k, m, sums):
                act.wait_ge(*sums)
                if not (isinstance(k.i, int) and k.value < 1):
                    act.wait_ge(hidden_ready, 2 * k.value)
                act.activation(tile_sums[0:F_EDGE, :].rearrange("f (j p) -> f p j", j=2),
                               agg[:, bass.ds(tile_node0(m), TILE)].rearrange("f (p j) -> f p j", j=2),
                               ACT.Copy).then_inc(tile_high_ready, 1)

            def copy_out(k):
                act.wait_ge(out_ready, k.plus(1).value)
                if not (isinstance(k.i, int) and k.value < 1):
                    act.wait_ge(out_added, k.value)
                act.activation(mlp_out[:, :, :].rearrange("p j f -> p (j f)"), out_bank[:, 0:TILE], ACT.Copy)\
                   .then_inc(out_copied, 1)

            def relu_hidden(k):
                if not (isinstance(k.i, int) and k.value < 1):
                    act.wait_ge(out_ready, k.value)
                for c in range(2):
                    act.wait_ge(hidden_ready, 2 * k.value + c + 1)
                    act.activation(hidden[:, c, :], hidden_bank[c][:, 0:TILE], ACT.Relu,
                                   bias=hidden_bias[:, c:c + 1]).then_inc(hidden_copied, 1)

            def step(s):
                early = isinstance(s.i, int)
                if not (early and s.value < 1):
                    copy_sums(s.plus(-1))
                if early:
                    for n in setup_batches(s.value):
                        copy_rel(n)
                if not (early and s.value < LAG + 1):
                    copy_out(s.plus(-LAG - 1))
                if not (early and s.value < LAG):
                    k = s.plus(-LAG)
                    tile_high(k, k, sums_of(k))
                    copy_turned(k)
                if not (early and (s.value < LAG - 1)):
                    deviate(s.plus(1 - LAG))
                if not (early and s.value < LAG):
                    relu_hidden(s.plus(-LAG))
                if not (early and (s.value < LAG - 1)):
                    normalise(s.plus(1 - LAG))

            act.wait_ge(eps_ready, 1)
            act.activation(deviation[:, 0:1], eps_col[:, :], ACT.Sqrt).then_inc(setup_scalar, 1)
            act.wait_ge(setup_scalar, 1)
            for n in range(2):
                copy_rel(n)
            act.wait_ge(zeros_ready, 1)
            for n in (2, 3):
                columns = agg[:, n * quarter:(n + 1) * quarter]
                act.activation(columns, zeros[:, 0:1].to_broadcast([F_EDGE, quarter]), ACT.Copy)\
                   .then_inc(agg_zeroed, 1)
            act.wait_ge(position_turned, 1)
            act.activation(position[:, :], out_bank[:, 0:3 * steps], ACT.Copy).then_inc(position_ready, 1)
            act.wait_ge(stacks_zeroed, 6)
            for s in range(LAG + 2):
                step(At(s))
                if s == 2:
                    act.wait_ge(bias_summed, 1)
                    act.wait_ge(weights_in, 9 * 16)
                    for c in range(2):
                        act.activation(hidden_bias[:, c:c + 1], turned_bank[:, c:c + 1], ACT.Identity,
                                       bias=b1_col[:, c:c + 1]).then_inc(bias_ready, 1)
                    act.activation(w1_high[:, :], w1_edge[:, :], ACT.Copy).then_inc(w1_high_ready, 1)
            pairs(act, LAG + 2, steps - 3 - LAG, step)
            step(At(steps - 1))
            copy_sums(At(steps - 1))
            for k in range(tiles - LAG, tiles):
                copy_turned(At(k))
                copy_out(At(k - 1))
                tile_high(At(k), At(k), sums_of(At(k)))
                if k + 1 < tiles:
                    deviate(At(k + 1))
                    normalise(At(k + 1))
                relu_hidden(At(k))
            copy_out(At(tiles - 1))
            act.wait_ge(flag_ready, 1)
            flag = act.value_load(general_flag[0:1, 0:1], min_val=0, max_val=1)
            with act.If(flag > 0):
                def tile(m):
                    k = m.plus(tiles)
                    deviate(k)
                    normalise(k)
                    copy_turned(k)
                    tile_high(k, m, (general_added, 2 * blocks_g + 1))
                    relu_hidden(k)
                    copy_out(k)

                pairs(act, 0, tiles, tile)

        @block.vector
        def _(dve):
            chain = [0]

            def link(ins):
                chain[0] += 1
                ins.then_inc(setup_chain, 1)
                dve.wait_ge(setup_chain, chain[0])

            def relative(b):
                rows = min(P, n_groups - b * P)
                n = (b * P < n_groups - GROUPS) + 3 * (b == blocks - 1)
                dve.wait_ge(dst_in[b], 16 * n)
                dve.tensor_scalar(rel_rows[0:rows, b, :], dst_rows[0:rows, b, 0:group_edges],
                                  dst_rows[0:rows, b, 0:1], None, ALU.subtract).then_inc(rel_rows_ready, 1)

            def check_sorted(b):
                rows = min(P, n_groups - b * P)
                link(dve.tensor_tensor_reduce(
                    out=order_scrap[0:rows, :], in0=dst_rows[0:rows, b, 0:group_edges],
                    in1=dst_rows[0:rows, b, 1:], scale=1.0, scalar=-1.0, op0=ALU.subtract, op1=ALU.max,
                    accum_out=violation[0:rows, b:b + 1]))

            def tables():
                dve.wait_ge(tables_in, 6 * 16)
                link(dve.memset(first_f[:, GROUPS:], 0.0))
                link(dve.tensor_copy(first_f[:, 0:GROUPS], first_i[:, :]))
                link(dve.tensor_copy(last_f[:, :], last_i[:, :]))
                link(dve.tensor_scalar(first_rel[:, :], first_f[:, :], first_f[:, 0:1], None, ALU.subtract))
                link(dve.tensor_scalar(last_rel[:, :], last_f[:, :], first_f[:, 0:1], None, ALU.subtract))
                link(dve.tensor_tensor(step_base_f[:, :], step_base_i[:, :], base_floor[:, :], ALU.max))
                link(dve.tensor_scalar(step_base[:, :], step_base_f[:, :], 0.0, float(nodes - 1), ALU.max, ALU.min))
                padded = first_rel[:, :].unsqueeze(2).to_broadcast([steps, 12, WINDOW])
                steps_ramp = ramp[0:steps, 0:WINDOW].unsqueeze(1).to_broadcast([steps, 12, WINDOW])
                dve.tensor_tensor(spread[:, :, :, :].rearrange("s q j w -> s (q j) w"), padded, steps_ramp,
                                  ALU.add).then_inc(spread_ready, 1)

            def check_windows():
                link(dve.tensor_tensor(tests[:, 0, :], last_rel[:, :], first_rel[:, 0:GROUPS], ALU.subtract))
                link(dve.tensor_scalar(tests[:, 0, :], tests[:, 0, :], float(1 - WINDOW), None, ALU.add))
                link(dve.tensor_tensor(tests[:, 1, :], low_limit[:, :], first_rel[:, 0:GROUPS], ALU.subtract))
                link(dve.tensor_tensor(tests[:, 2, :], last_rel[:, :], high_limit[:, :], ALU.subtract))
                link(dve.tensor_scalar(tests[:, 3, :], first_f[:, 0:GROUPS], final_node[:, 0:1], -1.0,
                                       ALU.subtract, ALU.mult))
                link(dve.tensor_scalar(tests[:, 4, :], last_f[:, :], float(1 - nodes), None, ALU.add))
                link(dve.tensor_scalar(tests[:, 5, :], first_f[:, 0:GROUPS], -1.0, None, ALU.mult))
                link(dve.tensor_reduce(violation[0:steps, blocks:], tests[:, :, :].rearrange("s a g -> s (a g)"),
                                       AX.X, ALU.max))
                dve.tensor_reduce(worst[:, :], violation[:, :], AX.X, ALU.max).then_inc(worst_ready, 1)

            def make_onehot(t, q):
                g0, ng = QUADS[q]
                if not (isinstance(t.i, int) and t.value < 2):
                    dve.wait_ge(edges_used, 3 * t.plus(-2).value + q + 1)
                cols = ng * EDGES_PER_ROW
                c0 = g0 * EDGES_PER_ROW
                dve.tensor_tensor(
                    onehot[t.parity][:, c0:c0 + cols, :],
                    rel[:, bass.ds(t.value * STEP_COLS + c0, cols)].unsqueeze(2).to_broadcast([P, cols, WINDOW]),
                    ramp[:, 0:WINDOW].unsqueeze(1).to_broadcast([P, cols, WINDOW]),
                    ALU.is_equal).then_inc(onehot_ready, 1)

            def make_placing(t):
                if not (isinstance(t.i, int) and t.value < 2):
                    dve.wait_ge(window_ready, t.plus(-1).value)
                for q, (low, high) in enumerate(QUAD_WINDOW):
                    rows = QUADS[q][1] * WINDOW
                    dve.tensor_scalar(placing[t.parity][0:rows, q, 0:high - low], ramp[0:rows, low:high],
                                      position[0:rows, bass.ds(t.value + q * steps, 1)], None,
                                      ALU.is_equal).then_inc(placing_ready, 1)

            def add_window(t):
                base = dve.value_load(step_base[0:1, bass.ds(t.value, 1)], min_val=0, max_val=nodes - 1)
                place = agg[:, bass.ds(base, STEP_WINDOW)]
                dve.wait_ge(window_ready, t.plus(1).value)
                if not (isinstance(t.i, int) and t.value < 1):
                    dve.wait_ge(agg_added, t.value)
                dve.tensor_tensor(place, place, window_bank[t.parity][0:F_EDGE, 0:STEP_WINDOW], ALU.add)\
                    .then_inc(agg_added, 1)

            def moments(k):
                dve.wait_ge(x_in[k.parity], k.half * 16 + 16)
                if not (isinstance(k.i, int) and k.value < 1):
                    dve.wait_ge(shift_ready, k.value)
                for j in range(2):
                    dve.bn_stats(bn6[:, j, :], x_buf[k.parity][:, j, :]).then_inc(moments_halfway, 1)

            def join_moments(k):
                for j in range(2):
                    dve.bn_aggr(mean_var[:, j, :], bn6[:, j, :]).then_inc(moments_ready, 1)

            def invert(k):
                dve.wait_ge(deviation_ready, k.plus(1).value)
                if not (isinstance(k.i, int) and k.value < 1):
                    dve.wait_ge(normed, k.value)
                dve.reciprocal(inverse[:, :], deviation[:, :]).then_inc(inverse_ready, 1)
                dve.wait_ge(inverse_ready, k.plus(1).value)
                dve.scalar_tensor_tensor(out=shift[:, :], in0=mean_var[:, :, 0], scalar=-1.0, in1=inverse[:, :],
                                         op0=ALU.mult, op1=ALU.mult).then_inc(shift_ready, 1)

            def tile_low(k, m):
                dve.wait_ge(tile_high_ready, k.plus(1).value)
                dve.tensor_tensor(tile_sums[STACK_LOW:STACK_LOW + F_EDGE, :].rearrange("f (j p) -> f p j", j=2),
                                  agg[:, bass.ds(tile_node0(m), TILE)].rearrange("f (p j) -> f p j", j=2),
                                  tile_sums[0:F_EDGE, :].bitcast(fp32).rearrange("f (j p) -> f p j", j=2),
                                  ALU.subtract).then_inc(tile_low_ready, 1)

            def step(s):
                early = isinstance(s.i, int)
                more = not (early and s.value + 1 >= steps)
                if more:
                    make_onehot(s.plus(1), 0)
                if not (early and s.value < LAG):
                    tile_low(s.plus(-LAG), s.plus(-LAG))
                if not (early and s.value < LAG - 1):
                    moments(s.plus(1 - LAG))
                if not (early and s.value < LAG - 1):
                    dve.wait_ge(moments_halfway, 2 * s.plus(1 - LAG).value + 2)
                if more:
                    make_onehot(s.plus(1), 1)
                if not (early and s.value < LAG - 1):
                    join_moments(s.plus(1 - LAG))
                if not (early and s.value < 1):
                    add_window(s.plus(-1))
                if not (early and s.value < LAG - 1):
                    invert(s.plus(1 - LAG))
                if more:
                    make_onehot(s.plus(1), 2)
                make_placing(s)

            relative(0)
            dve.wait_ge(consts_ready, 10)
            dve.wait_ge(rel_ready, 2)
            for q in range(3):
                make_onehot(At(0), q)
                if q == 0:
                    tables()
            if blocks > 1:
                relative(1)
            for s in range(LAG + 3):
                if s == 0:
                    dve.wait_ge(position_ready, 1)
                if s == 1:
                    dve.wait_ge(agg_zeroed, 4)
                step(At(s))
                if s == 0:
                    for b in range(2, blocks):
                        relative(b)
                if 0 < s <= blocks:
                    check_sorted(s - 1)
                if s == LAG - 1:
                    dve.wait_ge(w1_high_ready, 1)
                    dve.tensor_tensor(w1_low[:, :], w1_edge[:, :], w1_high[:, :].bitcast(fp32), ALU.subtract)\
                       .then_inc(w1_split, 1)
                if s == LAG + 1:
                    dve.wait_ge(rel_ready, 2 * blocks)
                    last_cols = (steps - 1) * STEP_COLS
                    link(dve.memset(rel[:, last_cols:last_cols + EDGES_PER_ROW], -1.0))
                    link(dve.memset(rel[0:masked_row, last_cols + EDGES_PER_ROW:last_cols + 2 * EDGES_PER_ROW],
                                    -1.0))
            pairs(dve, LAG + 3, steps - 4 - LAG, step)
            step(At(steps - 1))
            check_windows()
            moments(At(tiles - LAG + 1))
            dve.wait_ge(moments_halfway, 2 * (tiles - LAG + 1) + 2)
            join_moments(At(tiles - LAG + 1))
            invert(At(tiles - LAG + 1))
            tile_low(At(tiles - LAG), At(tiles - LAG))
            add_window(At(steps - 1))
            tile_low(At(tiles - LAG + 1), At(tiles - LAG + 1))
            moments(At(tiles - 1))
            dve.wait_ge(moments_halfway, 2 * tiles)
            join_moments(At(tiles - 1))
            invert(At(tiles - 1))
            tile_low(At(tiles - 1), At(tiles - 1))
            dve.wait_ge(worst_shared, 1)
            dve.tensor_scalar(general_flag[:, :], worst_all[0:1, :], 0.0, None, ALU.is_gt).then_inc(flag_ready, 1)

            dve.wait_ge(flag_ready, 1)
            flag = dve.value_load(general_flag[0:1, 0:1], min_val=0, max_val=1)
            with dve.If(flag > 0):
                dve.wait_ge(general_ramp_ready, 1)
                dve.sem_inc(general_staged, 1)
                dve.sem_inc(general_added, 1)

                def chunk(b, c, last):
                    n = b * steps + c
                    dve.wait_ge(general_dst_in, n * 16 + 16)
                    dve.wait_ge(general_staged, n * (2 * GROUPS) + 1)
                    dve.tensor_copy(general_rel[:, :], general_dst[:, :, :].rearrange("p g r -> p (g r)"))\
                        .then_inc(general_rel_chain, 1)
                    dve.wait_ge(general_rel_chain, n * 3 + 1)
                    if last:
                        dve.memset(general_rel[:, 0:EDGES_PER_ROW], -1.0).then_inc(general_rel_chain, 1)
                        dve.memset(general_rel[0:masked_row, EDGES_PER_ROW:2 * EDGES_PER_ROW], -1.0)\
                            .then_inc(general_rel_chain, 1)
                    else:
                        dve.sem_inc(general_rel_chain, 2)
                    with dve.Fori(0, GROUPS) as g:
                        dve.wait_ge(general_edges_in, n * 16 + 16)
                        dve.wait_ge(general_used, n * GROUPS + g + 1)
                        dve.tensor_copy(general_edges[:, :], edge_buf[0][:, :, :].rearrange("p g d -> p (g d)")
                                        [:, bass.ds(g * ROW, ROW)]).then_inc(general_staged, 1)
                        dve.wait_ge(general_rel_chain, n * 3 + 3)
                        dve.wait_ge(general_added, 2 * b + 1)
                        dve.tensor_tensor(
                            general_onehot[:, :, :],
                            general_rel[:, bass.ds(g * EDGES_PER_ROW, EDGES_PER_ROW)].unsqueeze(2)
                            .to_broadcast([P, EDGES_PER_ROW, GENERAL_BLOCK]),
                            general_ramp[:, :].unsqueeze(1).to_broadcast([P, EDGES_PER_ROW, GENERAL_BLOCK]),
                            ALU.is_equal).then_inc(general_staged, 1)

                with dve.Fori(0, blocks_g) as b:
                    with dve.Fori(0, steps - 1) as c:
                        chunk(b, c, False)
                    chunk(b, steps - 1, True)
                    dve.wait_ge(general_summed, b + 1)
                    dve.tensor_copy(agg[:, bass.ds(b * GENERAL_BLOCK, GENERAL_BLOCK)],
                                    window_bank[0][0:F_EDGE, 0:GENERAL_BLOCK]).then_inc(general_added, 1)
                    dve.wait_ge(general_added, 2 * b + 2)
                    dve.tensor_scalar(general_ramp[:, :], general_ramp[:, :], float(GENERAL_BLOCK), None,
                                      ALU.add).then_inc(general_added, 1)

                def tile(m):
                    k = m.plus(tiles)
                    moments(k)
                    dve.wait_ge(moments_halfway, 2 * k.value + 2)
                    dve.tensor_copy(general_rel[:, 0:1], eps_col[:, :])
                    join_moments(k)
                    invert(k)
                    tile_low(k, m)

                pairs(dve, 0, tiles, tile)

        @block.tensor
        def _(pe):
            def turn_rel(n):
                b, h = divmod(n, 2)
                rows = min(P, n_groups - b * P)
                pe.wait_ge(rel_rows_ready, b + 1)
                if n >= 2:
                    pe.wait_ge(rel_ready, n - 1)
                for r in range(3):
                    last = pe.transpose(
                        hidden_bank[h][:, r * P:r * P + rows],
                        rel_rows[0:rows, b, :].rearrange("g (p r) -> g r p", r=EDGES_PER_ROW)[:, 3 * h + r, :],
                        ident[0:rows, 0:rows])
                last.then_inc(rel_turned, 1)

            def sum_quad(t, q):
                g0, ng = QUADS[q]
                p = t.parity
                pe.wait_ge(edges_in[p][q], t.half * 16 + 16)
                pe.wait_ge(onehot_ready, 3 * t.value + q + 1)
                if q == 0 and not (isinstance(t.i, int) and t.value < 2):
                    pe.wait_ge(sums_copied, 4 * t.plus(-1).value)
                for pair in (range(0, 2), range(2, ng)):
                    for r in range(EDGES_PER_ROW):
                        for j in pair:
                            last = pe.matmul(
                                group_bank[p][WINDOW * j:WINDOW * (j + 1), q * F_EDGE:(q + 1) * F_EDGE],
                                onehot[p][:, (g0 + j) * EDGES_PER_ROW + r, :],
                                edge_buf[p][:, g0 + j, r * F_EDGE:(r + 1) * F_EDGE],
                                start=(r == 0), stop=(r == EDGES_PER_ROW - 1))
                last.then_inc(edges_used, 1)

            def place_sums(t):
                p = t.parity
                pe.wait_ge(sums_split, t.plus(1).value)
                pe.wait_ge(placing_ready, 3 * t.value + 3)
                if not (isinstance(t.i, int) and t.value < 2):
                    pe.wait_ge(agg_added, t.plus(-1).value)
                for q, (low, high) in enumerate(QUAD_WINDOW):
                    rows = QUADS[q][1] * WINDOW
                    for part in (0, LOW):
                        c0 = part + q * F_EDGE
                        last = pe.matmul(window_bank[p][0:2 * F_EDGE, low:high],
                                         split_sums[p][0:rows, c0:c0 + 2 * F_EDGE],
                                         placing[p][0:rows, q, 0:high - low],
                                         start=(q == 0 and part == 0), stop=(q == 2 and part == LOW),
                                         skip_group_check=True)
                last.then_inc(window_ready, 1)

            def turn_x(k):
                pe.wait_ge(normed, k.plus(1).value)
                if not (isinstance(k.i, int) and k.value < 1):
                    pe.wait_ge(turned_copied, k.value)
                for j in range(2):
                    last = pe.transpose(turned_bank[:, j * P:(j + 1) * P], normed_x[:, j, :], ident[:, :])
                last.then_inc(x_turned, 1)

            def first_layer(k):
                pe.wait_ge(turned_copied, k.plus(1).value)
                if not (isinstance(k.i, int) and k.value < 1):
                    pe.wait_ge(hidden_copied, 2 * k.value)
                for c in range(2):
                    pe.matmul(hidden_bank[c][:, 0:TILE], w1_node[:, c * P:(c + 1) * P], normed_t[:, :],
                              start=True, stop=False)
                    if c == 0:
                        pe.wait_ge(tile_low_ready, k.plus(1).value)
                    pe.matmul(hidden_bank[c][:, 0:TILE], w1_high[:, c * P:(c + 1) * P], tile_sums[:, :],
                              start=False, stop=False)
                    pe.matmul(hidden_bank[c][:, 0:TILE], w1_low[:, c * P:(c + 1) * P], tile_sums[:, :],
                              start=False, stop=True).then_inc(hidden_ready, 1)

            def second_layer(k):
                pe.wait_ge(hidden_copied, 2 * k.value + 2)
                if not (isinstance(k.i, int) and k.value < 1):
                    pe.wait_ge(out_copied, k.value)
                for j in range(2):
                    for c in range(2):
                        last = pe.matmul(out_bank[:, j * P:(j + 1) * P], hidden[:, c, j * P:(j + 1) * P],
                                         w2_sb[:, c, :], start=(c == 0), stop=(c == 1))
                last.then_inc(out_ready, 1)

            def turn_places():
                pe.wait_ge(spread_ready, 1)
                for q in range(3):
                    last = pe.transpose(out_bank[:, q * steps:(q + 1) * steps],
                                        spread[:, q, :, :].rearrange("s j w -> s (j w)"), ident[0:steps, 0:steps])
                last.then_inc(position_turned, 1)

            def sum_bias():
                pe.wait_ge(weights_in, 9 * 16)
                for c in range(2):
                    last = pe.matmul(turned_bank[:, c:c + 1], w1_global[:, c * P:(c + 1) * P], global_col[:, :],
                                     start=True, stop=True)
                last.then_inc(bias_summed, 1)

            def step(s):
                late = not (isinstance(s.i, int) and s.value < LAG)
                k = s.plus(-LAG)
                batches = list(setup_batches(s.value)) if isinstance(s.i, int) else []
                sum_quad(s, 0)
                if isinstance(s.i, int) and s.value == 0:
                    turn_places()
                if batches:
                    turn_rel(batches.pop(0))
                if late:
                    turn_x(k)
                sum_quad(s, 1)
                if not (isinstance(s.i, int) and s.value < 1):
                    place_sums(s.plus(-1))
                if batches:
                    turn_rel(batches.pop(0))
                if late:
                    first_layer(k)
                sum_quad(s, 2)
                if batches:
                    turn_rel(batches.pop(0))
                if isinstance(s.i, int) and s.value == 2:
                    sum_bias()
                if late:
                    second_layer(k)

            pe.wait_ge(ident_ready, 2)
            for n in range(2):
                turn_rel(n)
            for s in range(LAG + 2):
                if s == LAG:
                    pe.wait_ge(rel_ready, 2 * blocks)
                    pe.wait_ge(w1_split, 1)
                    pe.wait_ge(position_ready, 1)
                step(At(s))
            pairs(pe, LAG + 2, steps - 3 - LAG, step)
            step(At(steps - 1))
            turn_x(At(tiles - LAG))
            for k in range(tiles - LAG, tiles):
                first_layer(At(k))
                if k == tiles - LAG:
                    place_sums(At(steps - 1))
                if k + 1 < tiles:
                    turn_x(At(k + 1))
                second_layer(At(k))

            pe.wait_ge(flag_ready, 1)
            flag = pe.value_load(general_flag[0:1, 0:1], min_val=0, max_val=1)
            with pe.If(flag > 0):
                pe.wait_ge(zeros_ready, 1)
                pe.sem_inc(general_used, 1)
                bank_g = window_bank[0][0:F_EDGE, 0:GENERAL_BLOCK]

                def chunk(b, c):
                    with pe.Fori(0, GROUPS) as g:
                        n = (b * steps + c) * GROUPS + g
                        pe.wait_ge(general_staged, n * 2 + 3)
                        for r in range(EDGES_PER_ROW):
                            last = pe.matmul(bank_g, general_edges[:, r * F_EDGE:(r + 1) * F_EDGE],
                                             general_onehot[:, r, :], start=False, stop=False)
                        last.then_inc(general_used, 1)

                with pe.Fori(0, blocks_g) as b:
                    pe.wait_ge(general_added, b * 2 + 1)
                    pe.matmul(bank_g, zeros[0:1, 0:F_EDGE], zeros[0:1, :], start=True, stop=False)
                    with pe.Fori(0, steps - 1) as c:
                        chunk(b, c)
                    chunk(b, steps - 1)
                    pe.matmul(bank_g, zeros[0:1, 0:F_EDGE], zeros[0:1, :], start=False, stop=True)\
                        .then_inc(general_summed, 1)

                def tile(k):
                    turn_x(k)
                    first_layer(k)
                    second_layer(k)

                pairs(pe, tiles, tiles, tile)


_INS = ["x", "dst", "edge_attr_48", "L0_gnn_graph_globals", "L0_gnn_W1", "L0_gnn_b1", "L0_gnn_W2", "L0_gnn_b2"]


def kernel(**inputs):
    import numpy as _np
    import concourse.bacc as _bacc
    from concourse import mybir as _mybir
    from concourse.bass_utils import run_bass_kernel_spmd as _run

    nc = _bacc.Bacc("TRN2", target_bir_lowering=False, num_devices=1)
    arrays, args = {}, []
    for name in _INS:
        a = _np.ascontiguousarray(inputs[name])
        arrays[f"in_{name}"] = a
        args.append(nc.dram_tensor(f"in_{name}", a.shape, _mybir.dt.from_np(a.dtype), kind="ExternalInput").ap())
    shape = arrays["in_x"].shape
    args.append(nc.dram_tensor("out_0", shape, _mybir.dt.from_np(_np.dtype("float32")), kind="ExternalOutput").ap())
    gnn_kernel(nc, *args)
    return _run(nc, [arrays], core_ids=[0]).results[0]["out_0"]
```

```python
import concourse.bass as bass
from concourse import mybir
from contextlib import ExitStack

P = 128
EDGES_PER_ROW = 6
WINDOW = 32
GROUPS = 11
QUADS = ((0, 4), (4, 4), (8, 3))
QUAD_WINDOW = ((0, 104), (84, 196), (176, 276))
STEP_WINDOW = 276
TILE = 256
LAG = 2
F_NODE, F_EDGE, F_GLOBAL, HIDDEN = 128, 48, 64, 256
STACK, STACK_LOW = 112, 64
GENERAL_BLOCK = 512
EPS = 1e-5


class At:

    def __init__(self, c, i=0):
        self.c, self.i = c, i

    @property
    def value(self):
        return self.i * 2 + self.c if not isinstance(self.i, int) else self.c + 2 * self.i

    @property
    def parity(self):
        return self.c % 2

    @property
    def half(self):
        return self.i + self.c // 2

    def plus(self, n):
        return At(self.c + n, self.i)


def gnn_kernel(nc, x, dst, edges, graph_globals, w1, b1, w2, b2, out):
    fp32, fp32r, i32 = mybir.dt.float32, mybir.dt.float32r, mybir.dt.int32
    ALU = mybir.AluOpType
    ACT = mybir.ActivationFunctionType
    AX = mybir.AxisListType

    nodes, n_edges = x.shape[0], edges.shape[0]
    group_edges = P * EDGES_PER_ROW
    step_edges = group_edges * GROUPS
    steps = -(-n_edges // step_edges)
    tiles = -(-nodes // TILE)
    last_edge0 = n_edges - step_edges
    repeated = steps * step_edges - n_edges
    last_node0 = nodes - TILE
    fresh_row = (tiles * TILE - nodes) // 2
    masked_row = (repeated - group_edges) // EDGES_PER_ROW
    assert group_edges < repeated < 2 * group_edges and repeated % EDGES_PER_ROW == 0
    assert (tiles * TILE - nodes) % 2 == 0 and steps == tiles and steps % 2 == 1
    ROW = EDGES_PER_ROW * F_EDGE
    STEP_COLS = GROUPS * EDGES_PER_ROW
    n_groups = steps * GROUPS
    blocks = -(-n_groups // P)
    blocks_g = -(-nodes // GENERAL_BLOCK)
    agg_cols = -(-max(blocks_g * GENERAL_BLOCK, nodes + STEP_WINDOW) // 4) * 4
    quarter = agg_cols // 4

    ctx = ExitStack()
    with ctx:
        def sb(name, shape, dt=fp32):
            return ctx.enter_context(nc.sbuf_tensor(name, shape, dt))

        def bank(name):
            return ctx.enter_context(nc.psum_tensor(name, [P, 512], fp32))

        def sem(name):
            return ctx.enter_context(nc.semaphore(name))

        edge_buf = [sb(f"edge_buf{p}", [P, GROUPS, ROW]) for p in range(2)]
        onehot = [sb(f"onehot{p}", [P, STEP_COLS, WINDOW]) for p in range(2)]
        group_sums = [sb(f"group_sums{p}", [P, len(QUADS), F_EDGE]) for p in range(2)]
        split_sums = [sb(f"split_sums{p}", [P, len(QUADS), STACK], fp32r) for p in range(2)]
        placing = [sb(f"placing{p}", [P, 3, 112], fp32r) for p in range(2)]
        agg = sb("agg", [F_EDGE, agg_cols])
        dst_rows = sb("dst_rows", [P, blocks, group_edges + 1], i32)
        rel_rows = sb("rel_rows", [P, blocks, group_edges])
        order_scrap = sb("order_scrap", [P, group_edges])
        rel = sb("rel", [P, blocks * P * EDGES_PER_ROW])
        ends_i = sb("ends_i", [steps, GROUPS, 2], i32)
        first_f = sb("first_f", [steps, GROUPS + 1])
        last_f = sb("last_f", [steps, GROUPS])
        first_rel = sb("first_rel", [steps, GROUPS + 1])
        last_rel = sb("last_rel", [steps, GROUPS])
        tests = sb("tests", [steps, 6, GROUPS])
        low_limit = sb("low_limit", [steps, GROUPS])
        high_limit = sb("high_limit", [steps, GROUPS])
        final_node = sb("final_node", [steps, 1])
        spread = sb("spread", [steps, 3, 4, WINDOW])
        position = sb("position", [P, 3 * steps])
        step_base_i = sb("step_base_i", [1, steps], i32)
        step_base_f = sb("step_base_f", [1, steps])
        base_floor = sb("base_floor", [1, steps])
        step_base = sb("step_base", [1, steps], i32)
        violation = sb("violation", [P, blocks + 1])
        worst = sb("worst", [P, 1])
        worst_all = sb("worst_all", [P, 1])
        general_flag = sb("general_flag", [1, 1], i32)
        ramp = sb("ramp", [P, STEP_WINDOW])
        ones = sb("ones", [P, P])
        ident = sb("ident", [P, P])
        zeros = sb("zeros", [F_EDGE, GENERAL_BLOCK])
        w1_node = sb("w1_node", [F_NODE, HIDDEN])
        w1_edge = sb("w1_edge", [STACK, HIDDEN])
        w1_high = sb("w1_high", [STACK, HIDDEN], fp32r)
        w1_low = sb("w1_low", [STACK, HIDDEN], fp32r)
        tile_sums = [sb(f"tile_sums{p}", [STACK, TILE], fp32r) for p in range(2)]
        w1_global = sb("w1_global", [F_GLOBAL, HIDDEN])
        w2_sb = sb("w2_sb", [P, 2, F_NODE])
        global_col = sb("global_col", [F_GLOBAL, 1])
        b1_col = sb("b1_col", [P, 2])
        hidden_bias = sb("hidden_bias", [P, 2])
        b2_rows = sb("b2_rows", [P, 2, F_NODE])
        eps_col = sb("eps_col", [P, 1])
        x_buf = [sb(f"x_buf{p}", [P, 2, F_NODE]) for p in range(2)]
        xb_buf = [sb(f"xb_buf{p}", [P, 2, F_NODE]) for p in range(2)]
        out_buf = [sb(f"out_buf{p}", [P, 2, F_NODE]) for p in range(2)]
        bn6 = sb("bn6", [P, 2, 6])
        mean_var = sb("mean_var", [P, 2, 2])
        deviation = sb("deviation", [P, 2])
        inverse = sb("inverse", [P, 2])
        shift = sb("shift", [P, 2])
        normed_x = [sb(f"normed_x{p}", [P, 2, F_NODE]) for p in range(2)]
        normed_t = [sb(f"normed_t{p}", [P, TILE]) for p in range(2)]
        hidden = sb("hidden", [P, 2, TILE])
        last_hidden = sb("last_hidden", [P, 2, TILE])
        mlp_out = sb("mlp_out", [P, 2, F_NODE])
        general_edges = sb("general_edges", [P, ROW])
        general_dst = sb("general_dst", [P, GROUPS, EDGES_PER_ROW], i32)
        general_rel = sb("general_rel", [P, STEP_COLS])
        general_onehot = sb("general_onehot", [P, EDGES_PER_ROW, GENERAL_BLOCK])
        general_ramp = sb("general_ramp", [P, GENERAL_BLOCK])

        group_bank = [bank(f"group_bank{p}") for p in range(2)]
        window_bank = [bank(f"window_bank{p}") for p in range(2)]
        turned_bank, out_bank = bank("turned_bank"), bank("out_bank")
        hidden_bank = [bank(f"hidden_bank{c}") for c in range(2)]

        dst_in = [sem(f"dst_in{b}") for b in range(blocks)]
        tables_in = sem("tables_in")
        bases_in = sem("bases_in")
        weights_in = sem("weights_in")
        edges_in = [[sem(f"edges_in{p}{q}") for q in range(3)] for p in range(2)]
        x_in = [sem(f"x_in{p}") for p in range(2)]
        stored = [sem(f"stored{p}") for p in range(2)]
        consts_ready = sem("consts_ready")
        eps_ready = sem("eps_ready")
        ident_ready = sem("ident_ready")
        zeros_ready = sem("zeros_ready")
        agg_zeroed = sem("agg_zeroed")
        rel_rows_ready = sem("rel_rows_ready")
        rel_turned = sem("rel_turned")
        rel_ready = sem("rel_ready")
        tables_ready = sem("tables_ready")
        spread_ready = sem("spread_ready")
        position_turned = sem("position_turned")
        position_ready = sem("position_ready")
        bias_summed = sem("bias_summed")
        bias_ready = sem("bias_ready")
        setup_chain = sem("setup_chain")
        setup_scalar = sem("setup_scalar")
        onehot_ready = sem("onehot_ready")
        edges_used = sem("edges_used")
        sums_copied = sem("sums_copied")
        placing_ready = sem("placing_ready")
        window_ready = sem("window_ready")
        high_added = sem("high_added")
        agg_added = sem("agg_added")
        moments_halfway = sem("moments_halfway")
        moments_ready = sem("moments_ready")
        deviation_ready = sem("deviation_ready")
        inverse_ready = sem("inverse_ready")
        shift_ready = sem("shift_ready")
        normed = sem("normed")
        x_turned = sem("x_turned")
        turned_copied = sem("turned_copied")
        hidden_ready = sem("hidden_ready")
        hidden_copied = sem("hidden_copied")
        out_ready = sem("out_ready")
        xb_ready = sem("xb_ready")
        out_copied = sem("out_copied")
        out_added = sem("out_added")
        last_added = sem("last_added")
        stacks_zeroed = sem("stacks_zeroed")
        w1_high_ready = sem("w1_high_ready")
        w1_split = sem("w1_split")
        sums_split = sem("sums_split")
        tile_high_ready = sem("tile_high_ready")
        tile_low_ready = sem("tile_low_ready")
        worst_ready = sem("worst_ready")
        worst_shared = sem("worst_shared")
        flag_ready = sem("flag_ready")
        general_ramp_ready = sem("general_ramp_ready")
        general_edges_in = sem("general_edges_in")
        general_dst_in = sem("general_dst_in")
        general_rel_chain = sem("general_rel_chain")
        general_rel_ready = sem("general_rel_ready")
        general_staged = sem("general_staged")
        general_used = sem("general_used")
        general_summed = sem("general_summed")
        general_added = sem("general_added")

        edge_view = edges.rearrange("e d -> (e d)")

        def tile_node0(m):
            if isinstance(m.i, int) and m.value == tiles - 1:
                return last_node0
            return m.value * TILE

        def step_edge0(t):
            if isinstance(t.i, int) and t.value == steps - 1:
                return last_edge0
            return t.value * step_edges

        def pairs(eng, first, count, body):
            if count >= 2:
                with eng.Fori(0, count // 2) as i:
                    body(At(first, i))
                    body(At(first + 1, i))
            if count % 2:
                body(At(first + count - 1))

        ctx.enter_context(nc.allow_non_contiguous_dma(reason="a few small columns of dst, biases"))
        def sums_of(k):
            if isinstance(k.i, int) and k.value + 2 > steps:
                return agg_added, steps
            return agg_added, k.plus(2).value

        def turned_block(s):
            b = (s - LAG) // 2
            return b if s > LAG and (s - LAG) % 2 == 0 and b < blocks else None

        peeled = max(LAG + 4, LAG + 2 * blocks - 1)
        assert steps > peeled + 1

        block = ctx.enter_context(nc.Block())

        @block.sync
        def _(sp):
            def load_dst(b):
                first = b * P * group_edges
                rows = min(P, n_groups - GROUPS - b * P)
                if rows > 0:
                    sp.dma_start(dst_rows[0:rows, b, :], bass.AP(
                        tensor=dst.tensor, offset=first, ap=[[group_edges, rows], [1, group_edges + 1]]))\
                        .then_inc(dst_in[b], 16)
                if b == blocks - 1:
                    rows = max(rows, 0)
                    sp.dma_start(dst_rows[rows:rows + GROUPS - 1, b, :], bass.AP(
                        tensor=dst.tensor, offset=last_edge0,
                        ap=[[group_edges, GROUPS - 1], [1, group_edges + 1]])).then_inc(dst_in[b], 16)
                    rows += GROUPS - 1
                    sp.dma_start(dst_rows[rows:rows + 1, b, 0:group_edges],
                                 dst[n_edges - group_edges:].rearrange("(g e) -> g e", g=1))\
                        .then_inc(dst_in[b], 16)
                    sp.dma_start(dst_rows[rows:rows + 1, b, group_edges:],
                                 dst[n_edges - 1:].rearrange("(g e) -> g e", e=1)).then_inc(dst_in[b], 16)

            def load_edges(t):
                e0 = step_edge0(t)
                for q, (g0, ng) in enumerate(QUADS):
                    if not (isinstance(t.i, int) and t.value < 2):
                        sp.wait_ge(edges_used, 3 * t.plus(-2).value + q + 1)
                    n = ng * group_edges * F_EDGE
                    src = edge_view[bass.ds((e0 + g0 * group_edges) * F_EDGE, n)]
                    sp.dma_start(edge_buf[t.parity][:, g0:g0 + ng, :],
                                 src.rearrange("(g p d) -> p g d", g=ng, p=P))\
                      .then_inc(edges_in[t.parity][q], 16)

            def load_x(k, m):
                if not (isinstance(k.i, int) and k.value < 2):
                    sp.wait_ge(normed, k.plus(-1).value)
                    sp.wait_ge(xb_ready, k.plus(-1).value)
                sp.dma_start(x_buf[k.parity][:, :, :], x[bass.ds(tile_node0(m), TILE), :]
                             .rearrange("(p j) f -> p j f", j=2)).then_inc(x_in[k.parity], 16)

            def store(k, m):
                if isinstance(k.i, int) and k.value == tiles - 1:
                    sp.wait_ge(last_added, 1)
                else:
                    sp.wait_ge(out_added, k.plus(1).value)
                row = fresh_row if isinstance(m.i, int) and m.value == tiles - 1 else 0
                first = tile_node0(m) + 2 * row
                sp.dma_start(out[bass.ds(first, TILE - 2 * row), :].rearrange("(p j) f -> p j f", j=2),
                             out_buf[k.parity][row:, :, :]).then_inc(stored[k.parity], 16)

            load_dst(0)
            load_edges(At(0))
            load_edges(At(1))
            load_x(At(0), At(0))
            sp.wait_ge(stacks_zeroed, 1)
            for row in (0, STACK_LOW):
                sp.dma_start(w1_edge[row:row + F_EDGE, :], w1[F_NODE:F_NODE + F_EDGE, :]).then_inc(weights_in, 16)
            sp.dma_start(w1_node[:, :], w1[0:F_NODE, :]).then_inc(weights_in, 16)
            sp.dma_start(w2_sb[:, :, :], w2.rearrange("(c p) n -> p c n", p=P)).then_inc(weights_in, 16)
            sp.dma_start(w1_global[:, :], w1[F_NODE + F_EDGE:, :]).then_inc(weights_in, 16)
            sp.dma_start(global_col[:, :], graph_globals[0:1, :].rearrange("a g -> g a")).then_inc(weights_in, 16)
            sp.dma_start(b1_col[:, :], b1.rearrange("(c p) -> p c", p=P)).then_inc(weights_in, 16)
            for j in range(2):
                sp.dma_start(b2_rows[:, j, :], bass.AP(tensor=b2.tensor, offset=0, ap=[[0, P], [1, F_NODE]]))\
                    .then_inc(weights_in, 16)
            load_x(At(1), At(1))

            def step(s):
                if not (isinstance(s.i, int) and s.value < 4):
                    store(s.plus(-4), s.plus(-4))
                if not (isinstance(s.i, int) and (s.value < 2 or s.value >= tiles)):
                    load_x(s, s)
                if not (isinstance(s.i, int) and s.value + 2 >= steps):
                    load_edges(s.plus(2))
                if isinstance(s.i, int) and turned_block(s.value + 3) is not None:
                    load_dst(turned_block(s.value + 3))

            for s in range(peeled):
                step(At(s))
            pairs(sp, peeled, steps - 3 - peeled, step)
            for s in range(steps - 3, tiles + 4):
                step(At(s))
            sp.wait_ge(stored[0], 16 * ((tiles + 1) // 2))
            sp.wait_ge(stored[1], 16 * (tiles // 2))

            sp.wait_ge(flag_ready, 1)
            flag = sp.value_load(general_flag[0:1, 0:1], min_val=0, max_val=1)
            with sp.If(flag > 0):
                def load_chunk(b, c, edge0):
                    n = b * steps + c
                    sp.wait_ge(general_used, n * GROUPS + 1)
                    src = edge_view[bass.ds(edge0 * F_EDGE, step_edges * F_EDGE)]
                    sp.dma_start(edge_buf[0][:, :, :], src.rearrange("(g p d) -> p g d", g=GROUPS, p=P))\
                      .then_inc(general_edges_in, 16)
                    sp.dma_start(general_dst[:, :, :], dst[bass.ds(edge0, step_edges)]
                                 .rearrange("(g p r) -> p g r", g=GROUPS, p=P)).then_inc(general_dst_in, 16)

                with sp.Fori(0, blocks_g) as b:
                    with sp.Fori(0, steps - 1) as c:
                        load_chunk(b, c, c * step_edges)
                    load_chunk(b, steps - 1, last_edge0)

                def tile(m):
                    load_x(m.plus(tiles), m)
                    store(m.plus(tiles), m)

                pairs(sp, 0, tiles, tile)
                sp.wait_ge(stored[0], 16 * tiles)
                sp.wait_ge(stored[1], 16 * tiles)

        @block.gpsimd
        def _(pool):
            pool.memset(ones[:, :], 1.0).then_inc(ident_ready, 1)
            pool.wait_ge(ident_ready, 1)
            pool.affine_select(out=ident[:, :], in_=ones[:, :], compare_op=ALU.is_equal, fill=0.0,
                               base=0, pattern=[[-1, P]], channel_multiplier=1).then_inc(ident_ready, 1)
            pool.memset(eps_col[:, :], EPS).then_inc(eps_ready, 1)
            pool.iota(ramp[:, :], [[1, STEP_WINDOW]], base=0, channel_multiplier=0,
                      allow_small_or_imprecise_dtypes=True).then_inc(consts_ready, 1)
            pool.iota(final_node[:, :], [[0, 1]], base=-TILE, channel_multiplier=TILE,
                      allow_small_or_imprecise_dtypes=True).then_inc(consts_ready, 1)
            pool.iota(base_floor[:, :], [[TILE, steps]], base=-TILE, channel_multiplier=0,
                      allow_small_or_imprecise_dtypes=True).then_inc(consts_ready, 1)
            for (g0, ng), (low, high) in zip(QUADS, QUAD_WINDOW):
                pool.memset(low_limit[:, g0:g0 + ng], float(low)).then_inc(consts_ready, 1)
                pool.memset(high_limit[:, g0:g0 + ng], float(high - 1)).then_inc(consts_ready, 1)
            pool.memset(violation[:, :], 0.0).then_inc(consts_ready, 1)
            pool.dma_start(step_base_i[0:1, 0:steps - 1], bass.AP(
                tensor=dst.tensor, offset=0, ap=[[1, 1], [step_edges, steps - 1]])).then_inc(bases_in, 16)
            pool.dma_start(step_base_i[0:1, steps - 1:], bass.AP(
                tensor=dst.tensor, offset=last_edge0, ap=[[1, 1], [1, 1]])).then_inc(bases_in, 16)
            pool.memset(zeros[:, :], 0.0).then_inc(zeros_ready, 1)
            pool.memset(w1_edge[:, :], 0.0).then_inc(stacks_zeroed, 1)
            for p in range(2):
                pool.memset(tile_sums[p][:, :].bitcast(fp32), 0.0).then_inc(stacks_zeroed, 1)
                pool.memset(group_sums[p][:, :, :], 0.0).then_inc(stacks_zeroed, 1)
                pool.memset(split_sums[p][:, :, :].bitcast(fp32), 0.0).then_inc(stacks_zeroed, 1)
            for n in (1, 2):
                pool.memset(agg[:, n * quarter:(n + 1) * quarter], 0.0).then_inc(agg_zeroed, 1)

            def x_plus_b2(k):
                if isinstance(k.i, int) and k.value == 0:
                    pool.wait_ge(weights_in, 9 * 16)
                pool.wait_ge(x_in[k.parity], k.half * 16 + 16)
                if not (isinstance(k.i, int) and k.value < 2):
                    pool.wait_ge(out_added, k.plus(-1).value)
                pool.tensor_tensor(xb_buf[k.parity][:, :, :], x_buf[k.parity][:, :, :], b2_rows[:, :, :],
                                   ALU.add).then_inc(xb_ready, 1)

            def split_low(t):
                if isinstance(t.i, int) and t.value == 0:
                    pool.wait_ge(stacks_zeroed, 7)
                pool.wait_ge(sums_copied, 4 * t.value + 4)
                p = t.parity
                pool.tensor_tensor(split_sums[p][:, :, STACK_LOW:], group_sums[p][:, :, :],
                                   split_sums[p][:, :, 0:F_EDGE].bitcast(fp32), ALU.subtract).then_inc(sums_split, 1)

            def add_out(k):
                pool.wait_ge(out_copied, k.plus(1).value)
                pool.wait_ge(xb_ready, k.plus(1).value)
                if not (isinstance(k.i, int) and k.value < 2):
                    pool.wait_ge(stored[k.parity], k.half * 16)
                pool.tensor_tensor(out_buf[k.parity][:, :, :], mlp_out[:, :, :], xb_buf[k.parity][:, :, :],
                                   ALU.add).then_inc(out_added, 1)

            def step(s):
                early = isinstance(s.i, int)
                if not (early and s.value >= steps):
                    split_low(s)
                if not (early and s.value < LAG + 1):
                    add_out(s.plus(-LAG - 1))
                if not (early and not LAG - 1 <= s.value < tiles + LAG - 1):
                    x_plus_b2(s.plus(1 - LAG))

            for s in range(peeled):
                step(At(s))
            pairs(pool, peeled, steps - 1 - peeled, step)
            for s in range(steps - 1, tiles + LAG):
                step(At(s))
                if s == steps + 1:
                    pool.wait_ge(worst_ready, 1)
                    pool.partition_all_reduce(worst_all[:, :], worst[:, :], P, bass.bass_isa.ReduceOp.max)\
                        .then_inc(worst_shared, 1)
            pool.wait_ge(flag_ready, 1)
            flag = pool.value_load(general_flag[0:1, 0:1], min_val=0, max_val=1)
            with pool.If(flag > 0):
                pool.iota(general_ramp[:, :], [[1, GENERAL_BLOCK]], base=0, channel_multiplier=0,
                          allow_small_or_imprecise_dtypes=True).then_inc(general_ramp_ready, 1)

                def tile(k):
                    x_plus_b2(k)
                    add_out(k)

                pairs(pool, tiles, tiles, tile)

        @block.scalar
        def _(act):
            def copy_rel(n):
                b, h = divmod(n, 2)
                act.wait_ge(rel_turned, n + 1)
                rows = min(P, n_groups - b * P)
                dest = rel[:, b * P * EDGES_PER_ROW:(b * P + rows) * EDGES_PER_ROW]\
                    .rearrange("p (g r) -> p r g", r=EDGES_PER_ROW)[:, 3 * h:3 * h + 3, :]
                act.activation(dest, hidden_bank[h][:, 0:3 * P].rearrange("p (r g) -> p r g", r=3)[:, :, 0:rows],
                               ACT.Copy).then_inc(rel_ready, 1)

            def copy_sums(t):
                act.wait_ge(edges_used, 3 * t.value + 3)
                if not (isinstance(t.i, int) and t.value < 2):
                    act.wait_ge(window_ready, t.plus(-1).value)
                for rows, q0, q1 in ((P, 0, 2), (QUADS[2][1] * WINDOW, 2, 3)):
                    source = group_bank[t.parity][0:rows, q0 * F_EDGE:q1 * F_EDGE].rearrange("p (q f) -> p q f", f=F_EDGE)
                    for dest in (group_sums, split_sums):
                        act.activation(dest[t.parity][0:rows, q0:q1, 0:F_EDGE], source, ACT.Copy)\
                           .then_inc(sums_copied, 1)

            def deviate(k):
                act.wait_ge(moments_ready, 2 * k.value + 2)
                act.activation(deviation[:, :], mean_var[:, :, 1], ACT.Sqrt, bias=eps_col[:, :])\
                    .then_inc(deviation_ready, 1)

            def normalise(k):
                act.wait_ge(shift_ready, k.plus(1).value)
                if not (isinstance(k.i, int) and k.value < 2):
                    act.wait_ge(x_turned, k.plus(-1).value)
                act.activation(normed_x[k.parity][:, 0, :], x_buf[k.parity][:, 0, :], ACT.Relu,
                               bias=shift[:, 0:1], scale=inverse[:, 0:1])
                act.activation(normed_x[k.parity][:, 1, :], x_buf[k.parity][:, 1, :], ACT.Relu,
                               bias=shift[:, 1:2], scale=inverse[:, 1:2]).then_inc(normed, 1)

            def copy_turned(k):
                act.wait_ge(x_turned, k.plus(1).value)
                if not (isinstance(k.i, int) and k.value < 2):
                    act.wait_ge(hidden_ready, 2 * k.plus(-1).value)
                act.activation(normed_t[k.parity][:, :], turned_bank[:, 0:TILE], ACT.Copy).then_inc(turned_copied, 1)

            def tile_high(k, m, sums):
                act.wait_ge(*sums)
                if not (isinstance(k.i, int) and k.value < 2):
                    act.wait_ge(hidden_ready, 2 * k.plus(-1).value)
                act.activation(tile_sums[k.parity][0:F_EDGE, :].rearrange("f (j p) -> f p j", j=2),
                               agg[:, bass.ds(tile_node0(m), TILE)].rearrange("f (p j) -> f p j", j=2),
                               ACT.Copy).then_inc(tile_high_ready, 1)

            def copy_out(k):
                act.wait_ge(out_ready, k.plus(1).value)
                if not (isinstance(k.i, int) and k.value < 1):
                    act.wait_ge(out_added, k.value)
                act.activation(mlp_out[:, :, :].rearrange("p j f -> p (j f)"), out_bank[:, 0:TILE], ACT.Copy)\
                   .then_inc(out_copied, 1)

            def add_b1():
                act.wait_ge(bias_summed, 1)
                for c in range(2):
                    act.activation(hidden_bias[:, c:c + 1], out_bank[:, c:c + 1], ACT.Identity,
                                   bias=b1_col[:, c:c + 1]).then_inc(bias_ready, 1)
                act.wait_ge(bias_ready, 2)

            def relu_hidden(k, banks=hidden_bank, dest=hidden):
                if dest is hidden and not (isinstance(k.i, int) and k.value < 1):
                    act.wait_ge(out_ready, k.value)
                for c in range(2):
                    act.wait_ge(hidden_ready, 2 * k.value + c + 1)
                    act.activation(dest[:, c, :], banks[c][:, 0:TILE], ACT.Relu,
                                   bias=hidden_bias[:, c:c + 1]).then_inc(hidden_copied, 1)

            def step(s):
                early = isinstance(s.i, int)
                if early and s.value == LAG + 1:
                    add_b1()
                if not (early and s.value < LAG + 1):
                    relu_hidden(s.plus(-LAG - 1))
                if not (early and s.value < LAG):
                    copy_turned(s.plus(-LAG))
                if not (early and s.value < LAG):
                    tile_high(s.plus(-LAG), s.plus(-LAG), sums_of(s.plus(-LAG)))
                if not (early and s.value < LAG - 1):
                    deviate(s.plus(1 - LAG))
                    normalise(s.plus(1 - LAG))
                if early and turned_block(s.value) is not None:
                    for h in range(2):
                        copy_rel(2 * turned_block(s.value) + h)
                copy_sums(s)
                if not (early and s.value < LAG + 1):
                    copy_out(s.plus(-LAG - 1))

            ends = [[group_edges, GROUPS], [group_edges - 1, 2]]
            act.dma_start(ends_i[0:steps - 1, :, :], bass.AP(
                tensor=dst.tensor, offset=0, ap=[[step_edges, steps - 1]] + ends)).then_inc(tables_in, 16)
            act.dma_start(ends_i[steps - 1:steps, :, :], bass.AP(
                tensor=dst.tensor, offset=last_edge0, ap=[[1, 1]] + ends)).then_inc(tables_in, 16)
            act.wait_ge(eps_ready, 1)
            act.activation(deviation[:, 0:1], eps_col[:, :], ACT.Sqrt).then_inc(setup_scalar, 1)
            act.wait_ge(setup_scalar, 1)
            for n in range(2):
                copy_rel(n)
            act.wait_ge(zeros_ready, 1)
            act.activation(agg[:, 3 * quarter:], zeros[:, 0:1].to_broadcast([F_EDGE, quarter]), ACT.Copy)\
               .then_inc(agg_zeroed, 1)
            act.wait_ge(position_turned, 1)
            act.activation(position[:, :], out_bank[:, 0:3 * steps], ACT.Copy).then_inc(position_ready, 1)
            act.wait_ge(stacks_zeroed, 7)
            for s in range(peeled):
                step(At(s))
                if s == 1:
                    act.wait_ge(weights_in, 9 * 16)
                    act.activation(w1_high[:, :], w1_edge[:, :], ACT.Copy).then_inc(w1_high_ready, 1)
            pairs(act, peeled, steps - 1 - peeled, step)
            step(At(steps - 1))
            first, second, last = (At(k) for k in range(tiles - 3, tiles))
            deviate(last)
            relu_hidden(first)
            normalise(last)
            copy_turned(second)
            tile_high(second, second, sums_of(second))
            copy_out(first)
            copy_turned(last)
            tile_high(last, last, sums_of(last))
            relu_hidden(second)
            relu_hidden(last, group_bank, last_hidden)
            copy_out(second)
            act.wait_ge(flag_ready, 1)
            flag = act.value_load(general_flag[0:1, 0:1], min_val=0, max_val=1)
            with act.If(flag > 0):
                def tile(m):
                    k = m.plus(tiles)
                    deviate(k)
                    normalise(k)
                    copy_turned(k)
                    tile_high(k, m, (general_added, 2 * blocks_g + 1))
                    relu_hidden(k)
                    copy_out(k)

                pairs(act, 0, tiles, tile)

        @block.vector
        def _(dve):
            chain = [0]

            def link(ins):
                chain[0] += 1
                ins.then_inc(setup_chain, 1)
                dve.wait_ge(setup_chain, chain[0])

            def relative(b):
                rows = min(P, n_groups - b * P)
                n = (b * P < n_groups - GROUPS) + 3 * (b == blocks - 1)
                dve.wait_ge(dst_in[b], 16 * n)
                dve.tensor_scalar(rel_rows[0:rows, b, :], dst_rows[0:rows, b, 0:group_edges],
                                  dst_rows[0:rows, b, 0:1], None, ALU.subtract).then_inc(rel_rows_ready, 1)

            def check_sorted(b):
                rows = min(P, n_groups - b * P)
                link(dve.tensor_tensor_reduce(
                    out=order_scrap[0:rows, :], in0=dst_rows[0:rows, b, 0:group_edges],
                    in1=dst_rows[0:rows, b, 1:], scale=1.0, scalar=-1.0, op0=ALU.subtract, op1=ALU.max,
                    accum_out=violation[0:rows, b:b + 1]))

            def tables():
                dve.wait_ge(tables_in, 2 * 16)
                link(dve.memset(first_f[:, GROUPS:], 0.0))
                link(dve.tensor_copy(first_f[:, 0:GROUPS], ends_i[:, :, 0]))
                link(dve.tensor_copy(last_f[:, :], ends_i[:, :, 1]))
                link(dve.tensor_scalar(first_rel[:, :], first_f[:, :], first_f[:, 0:1], None, ALU.subtract))
                link(dve.tensor_scalar(last_rel[:, :], last_f[:, :], first_f[:, 0:1], None, ALU.subtract))
                padded = first_rel[:, :].unsqueeze(2).to_broadcast([steps, 12, WINDOW])
                steps_ramp = ramp[0:steps, 0:WINDOW].unsqueeze(1).to_broadcast([steps, 12, WINDOW])
                dve.tensor_tensor(spread[:, :, :, :].rearrange("s q j w -> s (q j) w"), padded, steps_ramp,
                                  ALU.add).then_inc(spread_ready, 1)

            def step_bases():
                dve.wait_ge(bases_in, 2 * 16)
                link(dve.tensor_tensor(step_base_f[:, :], step_base_i[:, :], base_floor[:, :], ALU.max))
                link(dve.tensor_scalar(step_base[:, :], step_base_f[:, :], 0.0, float(nodes - 1), ALU.max, ALU.min))

            def check_windows():
                link(dve.tensor_tensor(tests[:, 0, :], last_rel[:, :], first_rel[:, 0:GROUPS], ALU.subtract))
                link(dve.tensor_scalar(tests[:, 0, :], tests[:, 0, :], float(1 - WINDOW), None, ALU.add))
                link(dve.tensor_tensor(tests[:, 1, :], low_limit[:, :], first_rel[:, 0:GROUPS], ALU.subtract))
                link(dve.tensor_tensor(tests[:, 2, :], last_rel[:, :], high_limit[:, :], ALU.subtract))
                link(dve.tensor_scalar(tests[:, 3, :], first_f[:, 0:GROUPS], final_node[:, 0:1], -1.0,
                                       ALU.subtract, ALU.mult))
                link(dve.tensor_scalar(tests[:, 4, :], last_f[:, :], float(1 - nodes), None, ALU.add))
                link(dve.tensor_scalar(tests[:, 5, :], first_f[:, 0:GROUPS], -1.0, None, ALU.mult))
                link(dve.tensor_reduce(violation[0:steps, blocks:], tests[:, :, :].rearrange("s a g -> s (a g)"),
                                       AX.X, ALU.max))
                dve.tensor_reduce(worst[:, :], violation[:, :], AX.X, ALU.max).then_inc(worst_ready, 1)

            def make_onehot(t, q):
                g0, ng = QUADS[q]
                if not (isinstance(t.i, int) and t.value < 2):
                    dve.wait_ge(edges_used, 3 * t.plus(-2).value + q + 1)
                cols = ng * EDGES_PER_ROW
                c0 = g0 * EDGES_PER_ROW
                dve.tensor_tensor(
                    onehot[t.parity][:, c0:c0 + cols, :],
                    rel[:, bass.ds(t.value * STEP_COLS + c0, cols)].unsqueeze(2).to_broadcast([P, cols, WINDOW]),
                    ramp[:, 0:WINDOW].unsqueeze(1).to_broadcast([P, cols, WINDOW]),
                    ALU.is_equal).then_inc(onehot_ready, 1)

            def make_placing(t):
                if isinstance(t.i, int) and t.value == 0:
                    dve.wait_ge(position_ready, 1)
                if not (isinstance(t.i, int) and t.value < 2):
                    dve.wait_ge(window_ready, t.plus(-1).value)
                for q, (low, high) in enumerate(QUAD_WINDOW):
                    rows = QUADS[q][1] * WINDOW
                    dve.tensor_scalar(placing[t.parity][0:rows, q, 0:high - low], ramp[0:rows, low:high],
                                      position[0:rows, bass.ds(t.value + q * steps, 1)], None,
                                      ALU.is_equal).then_inc(placing_ready, 1)

            def add_window(t):
                base = dve.value_load(step_base[0:1, bass.ds(t.value, 1)], min_val=0, max_val=nodes - 1)
                place = agg[:, bass.ds(base, STEP_WINDOW)]
                dve.wait_ge(window_ready, t.plus(1).value)
                if not (isinstance(t.i, int) and t.value < 1):
                    dve.wait_ge(agg_added, t.value)
                dve.tensor_tensor(place, place, window_bank[t.parity][0:F_EDGE, 0:STEP_WINDOW], ALU.add)\
                    .then_inc(high_added, 1)
                dve.wait_ge(high_added, t.plus(1).value)
                dve.tensor_tensor(place, place, window_bank[t.parity][STACK_LOW:STACK, 0:STEP_WINDOW], ALU.add)\
                    .then_inc(agg_added, 1)

            def moments(k):
                dve.wait_ge(x_in[k.parity], k.half * 16 + 16)
                if not (isinstance(k.i, int) and k.value < 1):
                    dve.wait_ge(shift_ready, k.value)
                for j in range(2):
                    dve.bn_stats(bn6[:, j, :], x_buf[k.parity][:, j, :]).then_inc(moments_halfway, 1)

            def join_moments(k):
                for j in range(2):
                    dve.bn_aggr(mean_var[:, j, :], bn6[:, j, :]).then_inc(moments_ready, 1)

            def invert(k):
                dve.wait_ge(deviation_ready, k.plus(1).value)
                if not (isinstance(k.i, int) and k.value < 1):
                    dve.wait_ge(normed, k.value)
                dve.reciprocal(inverse[:, :], deviation[:, :]).then_inc(inverse_ready, 1)
                dve.wait_ge(inverse_ready, k.plus(1).value)
                dve.scalar_tensor_tensor(out=shift[:, :], in0=mean_var[:, :, 0], scalar=-1.0, in1=inverse[:, :],
                                         op0=ALU.mult, op1=ALU.mult).then_inc(shift_ready, 1)

            def tile_low(k, m):
                dve.wait_ge(tile_high_ready, k.plus(1).value)
                dve.tensor_tensor(tile_sums[k.parity][STACK_LOW:STACK_LOW + F_EDGE, :].rearrange("f (j p) -> f p j", j=2),
                                  agg[:, bass.ds(tile_node0(m), TILE)].rearrange("f (p j) -> f p j", j=2),
                                  tile_sums[k.parity][0:F_EDGE, :].bitcast(fp32).rearrange("f (j p) -> f p j", j=2),
                                  ALU.subtract).then_inc(tile_low_ready, 1)

            def step(s):
                early = isinstance(s.i, int)
                more = not (early and s.value + 1 >= steps)
                if not (early and s.value < LAG - 1):
                    moments(s.plus(1 - LAG))
                if not (early and s.value < 1):
                    add_window(s.plus(-1))
                if not (early and s.value < LAG - 1):
                    dve.wait_ge(moments_halfway, 2 * s.plus(1 - LAG).value + 2)
                if more:
                    make_onehot(s.plus(1), 0)
                if not (early and s.value < LAG - 1):
                    join_moments(s.plus(1 - LAG))
                if not (early and s.value < LAG):
                    tile_low(s.plus(-LAG), s.plus(-LAG))
                if not (early and s.value < LAG - 1):
                    invert(s.plus(1 - LAG))
                if more:
                    make_onehot(s.plus(1), 1)
                make_placing(s)
                if more:
                    make_onehot(s.plus(1), 2)

            dve.memset(agg[:, 0:quarter], 0.0).then_inc(agg_zeroed, 1)
            relative(0)
            dve.wait_ge(consts_ready, 10)
            dve.wait_ge(rel_ready, 2)
            make_onehot(At(0), 0)
            make_onehot(At(0), 1)
            tables()
            make_onehot(At(0), 2)
            for s in range(peeled):
                if s == LAG:
                    dve.wait_ge(w1_high_ready, 1)
                    dve.tensor_tensor(w1_low[:, :], w1_edge[:, :], w1_high[:, :].bitcast(fp32), ALU.subtract)\
                       .then_inc(w1_split, 1)
                if s == 1:
                    step_bases()
                    dve.wait_ge(agg_zeroed, 4)
                step(At(s))
                if turned_block(s + 1) is not None:
                    relative(turned_block(s + 1))
                if s >= LAG and (s - LAG) % 2 == 0 and (s - LAG) // 2 < blocks - 1:
                    check_sorted((s - LAG) // 2)
                if s == peeled - 1:
                    dve.wait_ge(rel_ready, 2 * blocks)
                    last_cols = (steps - 1) * STEP_COLS
                    link(dve.memset(rel[:, last_cols:last_cols + EDGES_PER_ROW], -1.0))
                    link(dve.memset(rel[0:masked_row, last_cols + EDGES_PER_ROW:last_cols + 2 * EDGES_PER_ROW],
                                    -1.0))
            pairs(dve, peeled, steps - 1 - peeled, step)
            step(At(steps - 1))

            second, last = At(tiles - 2), At(tiles - 1)
            moments(last)
            dve.wait_ge(moments_halfway, 2 * tiles)
            join_moments(last)
            invert(last)
            add_window(At(steps - 1))
            tile_low(second, second)
            tile_low(last, last)
            check_sorted(blocks - 1)
            check_windows()
            dve.wait_ge(out_ready, tiles)
            dve.wait_ge(xb_ready, tiles)
            dve.wait_ge(stored[last.parity], last.half * 16)
            dve.tensor_tensor(out_buf[last.parity][:, :, :], turned_bank[:, 0:TILE].rearrange("p (j f) -> p j f", j=2),
                              xb_buf[last.parity][:, :, :], ALU.add).then_inc(last_added, 1)
            dve.wait_ge(worst_shared, 1)
            dve.tensor_scalar(general_flag[:, :], worst_all[0:1, :], 0.0, None, ALU.is_gt).then_inc(flag_ready, 1)

            dve.wait_ge(flag_ready, 1)
            flag = dve.value_load(general_flag[0:1, 0:1], min_val=0, max_val=1)
            with dve.If(flag > 0):
                dve.wait_ge(general_ramp_ready, 1)
                dve.sem_inc(general_staged, 1)
                dve.sem_inc(general_added, 1)
                for p in range(2):
                    dve.wait_ge(stored[p], 16 * ((tiles + 1 - p) // 2))
                dve.sem_inc(out_copied, 1)
                dve.sem_inc(out_added, 1)

                def chunk(b, c, last):
                    n = b * steps + c
                    dve.wait_ge(general_dst_in, n * 16 + 16)
                    dve.wait_ge(general_staged, n * (2 * GROUPS) + 1)
                    dve.tensor_copy(general_rel[:, :], general_dst[:, :, :].rearrange("p g r -> p (g r)"))\
                        .then_inc(general_rel_chain, 1)
                    dve.wait_ge(general_rel_chain, n * 3 + 1)
                    if last:
                        dve.memset(general_rel[:, 0:EDGES_PER_ROW], -1.0).then_inc(general_rel_chain, 1)
                        dve.memset(general_rel[0:masked_row, EDGES_PER_ROW:2 * EDGES_PER_ROW], -1.0)\
                            .then_inc(general_rel_chain, 1)
                    else:
                        dve.sem_inc(general_rel_chain, 2)
                    with dve.Fori(0, GROUPS) as g:
                        dve.wait_ge(general_edges_in, n * 16 + 16)
                        dve.wait_ge(general_used, n * GROUPS + g + 1)
                        dve.tensor_copy(general_edges[:, :], edge_buf[0][:, :, :].rearrange("p g d -> p (g d)")
                                        [:, bass.ds(g * ROW, ROW)]).then_inc(general_staged, 1)
                        dve.wait_ge(general_rel_chain, n * 3 + 3)
                        dve.wait_ge(general_added, 2 * b + 1)
                        dve.tensor_tensor(
                            general_onehot[:, :, :],
                            general_rel[:, bass.ds(g * EDGES_PER_ROW, EDGES_PER_ROW)].unsqueeze(2)
                            .to_broadcast([P, EDGES_PER_ROW, GENERAL_BLOCK]),
                            general_ramp[:, :].unsqueeze(1).to_broadcast([P, EDGES_PER_ROW, GENERAL_BLOCK]),
                            ALU.is_equal).then_inc(general_staged, 1)

                with dve.Fori(0, blocks_g) as b:
                    with dve.Fori(0, steps - 1) as c:
                        chunk(b, c, False)
                    chunk(b, steps - 1, True)
                    dve.wait_ge(general_summed, b + 1)
                    dve.tensor_copy(agg[:, bass.ds(b * GENERAL_BLOCK, GENERAL_BLOCK)],
                                    window_bank[0][0:F_EDGE, 0:GENERAL_BLOCK]).then_inc(general_added, 1)
                    dve.wait_ge(general_added, 2 * b + 2)
                    dve.tensor_scalar(general_ramp[:, :], general_ramp[:, :], float(GENERAL_BLOCK), None,
                                      ALU.add).then_inc(general_added, 1)

                def tile(m):
                    k = m.plus(tiles)
                    moments(k)
                    dve.wait_ge(moments_halfway, 2 * k.value + 2)
                    dve.tensor_copy(general_rel[:, 0:1], eps_col[:, :])
                    join_moments(k)
                    invert(k)
                    tile_low(k, m)

                pairs(dve, 0, tiles, tile)

        @block.tensor
        def _(pe):
            def turn_rel(n):
                b, h = divmod(n, 2)
                rows = min(P, n_groups - b * P)
                pe.wait_ge(rel_rows_ready, b + 1)
                if n >= 2:
                    pe.wait_ge(rel_ready, n - 1)
                for r in range(3):
                    last = pe.transpose(
                        hidden_bank[h][:, r * P:r * P + rows],
                        rel_rows[0:rows, b, :].rearrange("g (p r) -> g r p", r=EDGES_PER_ROW)[:, 3 * h + r, :],
                        ident[0:rows, 0:rows])
                last.then_inc(rel_turned, 1)

            def sum_quad(t, q):
                g0, ng = QUADS[q]
                p = t.parity
                pe.wait_ge(edges_in[p][q], t.half * 16 + 16)
                pe.wait_ge(onehot_ready, 3 * t.value + q + 1)
                if q == 0 and not (isinstance(t.i, int) and t.value < 2):
                    pe.wait_ge(sums_copied, 4 * t.plus(-1).value)
                for r in range(EDGES_PER_ROW):
                    for j in range(ng):
                        last = pe.matmul(
                            group_bank[p][WINDOW * j:WINDOW * (j + 1), q * F_EDGE:(q + 1) * F_EDGE],
                            onehot[p][:, (g0 + j) * EDGES_PER_ROW + r, :],
                            edge_buf[p][:, g0 + j, r * F_EDGE:(r + 1) * F_EDGE],
                            start=(r == 0), stop=(r == EDGES_PER_ROW - 1))
                last.then_inc(edges_used, 1)

            def place_sums(t):
                p = t.parity
                pe.wait_ge(sums_split, t.plus(1).value)
                pe.wait_ge(placing_ready, 3 * t.value + 3)
                if not (isinstance(t.i, int) and t.value < 2):
                    pe.wait_ge(agg_added, t.plus(-1).value)
                for q, (low, high) in enumerate(QUAD_WINDOW):
                    rows = QUADS[q][1] * WINDOW
                    last = pe.matmul(window_bank[p][0:STACK, low:high], split_sums[p][0:rows, q, :],
                                     placing[p][0:rows, q, 0:high - low],
                                     start=(q == 0), stop=(q == 2), skip_group_check=True)
                last.then_inc(window_ready, 1)

            def turn_x(k):
                pe.wait_ge(normed, k.plus(1).value)
                if not (isinstance(k.i, int) and k.value < 1):
                    pe.wait_ge(turned_copied, k.value)
                for j in range(2):
                    last = pe.transpose(turned_bank[:, j * P:(j + 1) * P], normed_x[k.parity][:, j, :], ident[:, :])
                last.then_inc(x_turned, 1)

            def first_layer(k, banks=hidden_bank):
                pe.wait_ge(turned_copied, k.plus(1).value)
                if banks is hidden_bank and not (isinstance(k.i, int) and k.value < 1):
                    pe.wait_ge(hidden_copied, 2 * k.value)
                for c in range(2):
                    pe.matmul(banks[c][:, 0:TILE], w1_node[:, c * P:(c + 1) * P], normed_t[k.parity][:, :],
                              start=True, stop=False)
                    if c == 0:
                        pe.wait_ge(tile_low_ready, k.plus(1).value)
                    pe.matmul(banks[c][:, 0:TILE], w1_high[:, c * P:(c + 1) * P], tile_sums[k.parity][:, :],
                              start=False, stop=False)
                    pe.matmul(banks[c][:, 0:TILE], w1_low[:, c * P:(c + 1) * P], tile_sums[k.parity][:, :],
                              start=False, stop=True).then_inc(hidden_ready, 1)

            def second_layer(k, source=hidden, to_bank=out_bank):
                pe.wait_ge(hidden_copied, 2 * k.value + 2)
                if to_bank is out_bank and not (isinstance(k.i, int) and k.value < 1):
                    pe.wait_ge(out_copied, k.value)
                for j in range(2):
                    for c in range(2):
                        last = pe.matmul(to_bank[:, j * P:(j + 1) * P], source[:, c, j * P:(j + 1) * P],
                                         w2_sb[:, c, :], start=(c == 0), stop=(c == 1))
                last.then_inc(out_ready, 1)

            def turn_places():
                pe.wait_ge(spread_ready, 1)
                for q in range(3):
                    last = pe.transpose(out_bank[:, q * steps:(q + 1) * steps],
                                        spread[:, q, :, :].rearrange("s j w -> s (j w)"), ident[0:steps, 0:steps])
                last.then_inc(position_turned, 1)

            def sum_bias():
                pe.wait_ge(position_ready, 1)
                pe.wait_ge(weights_in, 9 * 16)
                for c in range(2):
                    last = pe.matmul(out_bank[:, c:c + 1], w1_global[:, c * P:(c + 1) * P], global_col[:, :],
                                     start=True, stop=True)
                last.then_inc(bias_summed, 1)

            def keep_clock(n, bank):
                halves = ones[:, :].bitcast(mybir.dt.bfloat16)
                for _ in range(n):
                    pe.matmul(bank[:, 0:2 * P], halves[:, 0:P], halves[:, :], start=True, stop=True)

            def sum_edges(s):
                early = isinstance(s.i, int)
                fill = early and s.value <= LAG
                sum_quad(s, 0)
                if fill:
                    keep_clock(5, hidden_bank[0])
                sum_quad(s, 1)
                if early and turned_block(s.value) is not None:
                    pe.wait_ge(hidden_copied, 2 * (s.value - LAG))
                    for h in range(2):
                        turn_rel(2 * turned_block(s.value) + h)
                if fill:
                    keep_clock(5, hidden_bank[0])
                if early and s.value == 0:
                    turn_places()
                    keep_clock(5, hidden_bank[0])
                sum_quad(s, 2)
                if fill:
                    keep_clock(5, hidden_bank[0])

            def step(s):
                early = isinstance(s.i, int)
                if not (early and s.value < LAG + 1):
                    second_layer(s.plus(-LAG - 1))
                if early and s.value == LAG:
                    pe.wait_ge(w1_split, 1)
                    sum_bias()
                if early and turned_block(s.value) is not None:
                    turn_x(s.plus(1 - LAG))
                    pe.wait_ge(rel_ready, 2 * turned_block(s.value) + 2)
                if not (early and s.value < LAG):
                    first_layer(s.plus(-LAG))
                if not (early and (s.value < LAG - 1 or turned_block(s.value) is not None)):
                    turn_x(s.plus(1 - LAG))
                place_sums(s)
                if not (early and s.value + 1 >= steps):
                    sum_edges(s.plus(1))

            pe.wait_ge(ident_ready, 2)
            keep_clock(14, turned_bank)
            for n in range(2):
                turn_rel(n)
            keep_clock(8, turned_bank)
            sum_edges(At(0))
            for s in range(peeled):
                step(At(s))
            pairs(pe, peeled, steps - 1 - peeled, step)
            step(At(steps - 1))
            first, second, last = (At(k) for k in range(tiles - 3, tiles))
            second_layer(first)
            turn_x(last)
            first_layer(second)
            first_layer(last, group_bank)
            second_layer(second)
            second_layer(last, last_hidden, turned_bank)

            pe.wait_ge(flag_ready, 1)
            flag = pe.value_load(general_flag[0:1, 0:1], min_val=0, max_val=1)
            with pe.If(flag > 0):
                pe.wait_ge(zeros_ready, 1)
                pe.sem_inc(general_used, 1)
                bank_g = window_bank[0][0:F_EDGE, 0:GENERAL_BLOCK]

                def chunk(b, c):
                    with pe.Fori(0, GROUPS) as g:
                        n = (b * steps + c) * GROUPS + g
                        pe.wait_ge(general_staged, n * 2 + 3)
                        for r in range(EDGES_PER_ROW):
                            last = pe.matmul(bank_g, general_edges[:, r * F_EDGE:(r + 1) * F_EDGE],
                                             general_onehot[:, r, :], start=False, stop=False)
                        last.then_inc(general_used, 1)

                with pe.Fori(0, blocks_g) as b:
                    pe.wait_ge(general_added, b * 2 + 1)
                    pe.matmul(bank_g, zeros[0:1, 0:F_EDGE], zeros[0:1, :], start=True, stop=False)
                    with pe.Fori(0, steps - 1) as c:
                        chunk(b, c)
                    chunk(b, steps - 1)
                    pe.matmul(bank_g, zeros[0:1, 0:F_EDGE], zeros[0:1, :], start=False, stop=True)\
                        .then_inc(general_summed, 1)

                def tile(k):
                    turn_x(k)
                    first_layer(k)
                    second_layer(k)

                pairs(pe, tiles, tiles, tile)


_INS = ["x", "dst", "edge_attr_48", "L0_gnn_graph_globals", "L0_gnn_W1", "L0_gnn_b1", "L0_gnn_W2", "L0_gnn_b2"]


def kernel(**inputs):
    import numpy as _np
    import concourse.bacc as _bacc
    from concourse import mybir as _mybir
    from concourse.bass_utils import run_bass_kernel_spmd as _run

    nc = _bacc.Bacc("TRN2", target_bir_lowering=False, num_devices=1)
    arrays, args = {}, []
    for name in _INS:
        a = _np.ascontiguousarray(inputs[name])
        arrays[f"in_{name}"] = a
        args.append(nc.dram_tensor(f"in_{name}", a.shape, _mybir.dt.from_np(a.dtype), kind="ExternalInput").ap())
    shape = arrays["in_x"].shape
    args.append(nc.dram_tensor("out_0", shape, _mybir.dt.from_np(_np.dtype("float32")), kind="ExternalOutput").ap())
    gnn_kernel(nc, *args)
    return _run(nc, [arrays], core_ids=[0]).results[0]["out_0"]
```
